# Optimizing a Trainium2 kernel written in Bass

```python
import numpy as np
import jax
import jax.numpy as jnp

def _softmax(x, axis=-1):
    return jax.nn.softmax(x, axis=axis)

def _gelu(x):
    return jax.nn.gelu(x, approximate=True)

def _silu(x):
    return jax.nn.silu(x)

def _sigmoid(x):
    return jax.nn.sigmoid(x)

def _layernorm(x, axis=-1, eps=1e-05):
    m = jnp.mean(x, axis=axis, keepdims=True)
    v = jnp.var(x, axis=axis, keepdims=True)
    return (x - m) / jnp.sqrt(v + eps)

def _scatter_add(tgt, idx, src, axis=0):
    return tgt.at[idx].add(src)

def _segment_sum(src, seg, n):
    return jax.ops.segment_sum(src, seg, n)
kernel_name = 'mk_adaln_attn_ffn_d1_seqx_r2_7b9f08'

def setup_inputs(seed: int=0):
    np.random.seed(seed)
    _w = jnp.asarray

    def _rec_inputs():
        import jax
        import jax.numpy as jnp
        _rk = jax.random.key(seed)
        x = 4.136e-05 + 0.9999 * jax.random.normal(jax.random.fold_in(_rk, 1), (64, 128, 512), jnp.float32)
        _lenS = 128 - jax.random.randint(jax.random.fold_in(_rk, 7), (64,), 0, max(1, 128 // 4) + 1, jnp.int32)
        _lenS2 = 128 - jax.random.randint(jax.random.fold_in(_rk, 8), (64,), 0, max(1, 128 // 4) + 1, jnp.int32)
        cond_1024 = -0.00608245 + 1.00131 * jax.random.normal(jax.random.fold_in(_rk, 11), (64, 512), jnp.float32)
        return (x, cond_1024)
    x, cond_1024 = _rec_inputs()

    def _L0_cond_setup():
        import jax, jax.numpy as jnp
        import numpy as np
        B, T, D_IN, V_IN, E = (64, 128, 512, 512, 512)
        key = jax.random.key(seed)
        ks = jax.random.split(key, 16)
        s = 0.01
        return {'video': jax.random.normal(ks[0], (B, V_IN), jnp.float32), 'seq': jax.random.normal(ks[1], (B, T, D_IN), jnp.float32), 'W_z': jax.random.normal(ks[2], (D_IN, E), jnp.float32) * s, 'U_z': jax.random.normal(ks[3], (E, E), jnp.float32) * s, 'C_z': jax.random.normal(ks[4], (V_IN, E), jnp.float32) * s, 'b_z': jnp.zeros((E,), jnp.float32), 'W_r': jax.random.normal(ks[5], (D_IN, E), jnp.float32) * s, 'U_r': jax.random.normal(ks[6], (E, E), jnp.float32) * s, 'C_r': jax.random.normal(ks[7], (V_IN, E), jnp.float32) * s, 'b_r': jnp.zeros((E,), jnp.float32), 'W': jax.random.normal(ks[8], (D_IN, E), jnp.float32) * s, 'U': jax.random.normal(ks[9], (E, E), jnp.float32) * s, 'C': jax.random.normal(ks[10], (V_IN, E), jnp.float32) * s, 'b': jnp.zeros((E,), jnp.float32)}
    _L0_cond_all = _L0_cond_setup()
    _L0_cond_in = {k: v for k, v in _L0_cond_all.items() if k in ('W_z', 'U_z', 'C_z', 'b_z', 'W_r', 'U_r', 'C_r', 'b_r', 'W', 'U', 'C', 'b')}
    del _L0_cond_all

    def _L0_attn_setup():
        import jax, jax.numpy as jnp
        import numpy as np
        BLOCK = 512

        def _block_cumsum_flat(x):
            shape = x.shape
            flat = x.reshape(-1, BLOCK)
            y = jnp.cumsum(flat, axis=-1)
            return y.reshape(shape)
        key = jax.random.key(seed)
        k1, k2, k3 = jax.random.split(key, 3)
        b, s, h = (8, 2048, 512)
        x = jax.random.normal(k1, (b, s, h), dtype=jnp.float32)
        bound = 1.0 / np.sqrt(h)
        W = jax.random.uniform(k2, (h, h), dtype=jnp.float32, minval=-bound, maxval=bound)
        bias = jax.random.uniform(k3, (h,), dtype=jnp.float32, minval=-bound, maxval=bound)
        return {'x': x, 'W': W, 'bias': bias}
    _L0_attn_all = _L0_attn_setup()
    _L0_attn_in = {k: v for k, v in _L0_attn_all.items() if k in ('W', 'bias')}
    del _L0_attn_all

    def _L0_cond2_setup():
        import jax, jax.numpy as jnp
        import numpy as np
        IN_FEATURES = 512
        OUT_FEATURES = 512
        BATCH = 32
        SEQ = 512
        EPS = 1e-08
        key = jax.random.key(seed)
        k1, k2, k3 = jax.random.split(key, 3)
        Efou = jax.random.normal(k1, (BATCH, SEQ, IN_FEATURES), dtype=jnp.float32)
        y = jax.random.normal(k2, (BATCH, IN_FEATURES), dtype=jnp.float32)
        weight = jax.random.normal(k3, (IN_FEATURES, OUT_FEATURES), dtype=jnp.float32)
        return {'Efou': Efou, 'y': y, 'weight': weight}
    _L0_cond2_all = _L0_cond2_setup()
    _L0_cond2_in = {k: v for k, v in _L0_cond2_all.items() if k in ('weight',)}
    del _L0_cond2_all

    def _L0_ffn_setup():
        import jax, jax.numpy as jnp
        import numpy as np
        DIM = 512

        def _reference_tuple_inner(x, W_r, W_k, W_v, mu_r, mu_k):
            B, T, C = x.shape
            x_prev = jnp.concatenate([jnp.zeros((B, 1, C), x.dtype), x[:, :-1, :]], axis=1)
            xr = mu_r * x + (1.0 - mu_r) * x_prev
            xk = mu_k * x + (1.0 - mu_k) * x_prev
            r = jax.nn.sigmoid(jnp.einsum('btc,dc->btd', xr, W_r))
            k = jnp.einsum('btc,dc->btd', xk, W_k)
            k_act = jnp.square(jax.nn.relu(k))
            out = r * jnp.einsum('btc,dc->btd', k_act, W_v)
            new_state = x[:, -1, :]
            return (out, new_state)
        key = jax.random.key(seed)
        ks = jax.random.split(key, 6)
        B, T, C = (8, 1024, DIM)
        x = jax.random.normal(ks[0], (B, T, C), dtype=jnp.float32)
        s = 1.0 / np.sqrt(C)
        W_r = jax.random.uniform(ks[1], (C, C), jnp.float32, -s, s)
        W_k = jax.random.uniform(ks[2], (C, C), jnp.float32, -s, s)
        W_v = jax.random.uniform(ks[3], (C, C), jnp.float32, -s, s)
        mu_r = jax.random.uniform(ks[4], (C,), jnp.float32)
        mu_k = jax.random.uniform(ks[5], (C,), jnp.float32)
        return {'x': x, 'W_r': W_r, 'W_k': W_k, 'W_v': W_v, 'mu_r': mu_r, 'mu_k': mu_k}
    _L0_ffn_all = _L0_ffn_setup()
    _L0_ffn_in = {k: v for k, v in _L0_ffn_all.items() if k in ('W_r', 'W_k', 'W_v', 'mu_r', 'mu_k')}
    del _L0_ffn_all
    return {'x': x, 'cond_1024': cond_1024, 'L0_cond_W_z': _L0_cond_in['W_z'], 'L0_cond_U_z': _L0_cond_in['U_z'], 'L0_cond_C_z': _L0_cond_in['C_z'], 'L0_cond_b_z': _L0_cond_in['b_z'], 'L0_cond_W_r': _L0_cond_in['W_r'], 'L0_cond_U_r': _L0_cond_in['U_r'], 'L0_cond_C_r': _L0_cond_in['C_r'], 'L0_cond_b_r': _L0_cond_in['b_r'], 'L0_cond_W': _L0_cond_in['W'], 'L0_cond_U': _L0_cond_in['U'], 'L0_cond_C': _L0_cond_in['C'], 'L0_cond_b': _L0_cond_in['b'], 'L0_attn_W': _L0_attn_in['W'], 'L0_attn_bias': _L0_attn_in['bias'], 'L0_cond2_weight': _L0_cond2_in['weight'], 'L0_ffn_W_r': _L0_ffn_in['W_r'], 'L0_ffn_W_k': _L0_ffn_in['W_k'], 'L0_ffn_W_v': _L0_ffn_in['W_v'], 'L0_ffn_mu_r': _L0_ffn_in['mu_r'], 'L0_ffn_mu_k': _L0_ffn_in['mu_k']}

def reference(x, cond_1024, L0_cond_W_z, L0_cond_U_z, L0_cond_C_z, L0_cond_b_z, L0_cond_W_r, L0_cond_U_r, L0_cond_C_r, L0_cond_b_r, L0_cond_W, L0_cond_U, L0_cond_C, L0_cond_b, L0_attn_W, L0_attn_bias, L0_cond2_weight, L0_ffn_W_r, L0_ffn_W_k, L0_ffn_W_v, L0_ffn_mu_r, L0_ffn_mu_k):
    import jax
    import jax.numpy as jnp

    def _L0_cond_ref(video, seq, W_z, U_z, C_z, b_z, W_r, U_r, C_r, b_r, W, U, C, b):
        import jax, jax.numpy as jnp
        import numpy as np
        B, T, D_IN, V_IN, E = (64, 128, 512, 512, 512)
        vz = video @ C_z + b_z
        vr = video @ C_r + b_r
        vh = video @ C + b
        xz = jnp.einsum('btd,de->bte', seq, W_z)
        xr = jnp.einsum('btd,de->bte', seq, W_r)
        xh = jnp.einsum('btd,de->bte', seq, W)

        def step(h, xs):
            xzt, xrt, xht = xs
            z = jax.nn.sigmoid(xzt + h @ U_z + vz)
            r = jax.nn.sigmoid(xrt + h @ U_r + vr)
            hh = jnp.tanh(xht + r * h @ U + vh)
            h_new = (1.0 - z) * h + z * hh
            return (h_new, h_new)
        h0 = jnp.zeros((seq.shape[0], U.shape[0]), seq.dtype)
        xs = (jnp.swapaxes(xz, 0, 1), jnp.swapaxes(xr, 0, 1), jnp.swapaxes(xh, 0, 1))
        _, out_t = jax.lax.scan(step, h0, xs)
        return jnp.swapaxes(out_t, 0, 1)

    def _L0_attn_ref(x, W, bias):
        import jax, jax.numpy as jnp
        import numpy as np
        BLOCK = 512

        def _block_cumsum_flat(x):
            shape = x.shape
            flat = x.reshape(-1, BLOCK)
            y = jnp.cumsum(flat, axis=-1)
            return y.reshape(shape)
        h = jnp.einsum('bsh,oh->bso', x, W) + bias
        return _block_cumsum_flat(h)

    def _L0_cond2_ref(Efou, y, weight):
        import jax, jax.numpy as jnp
        import numpy as np
        IN_FEATURES = 512
        OUT_FEATURES = 512
        BATCH = 32
        SEQ = 512
        EPS = 1e-08
        scale = 1.0 / np.sqrt(np.float32(weight.shape[0]))
        ys = y * scale
        d = jax.lax.rsqrt(jnp.einsum('bi,io->bo', ys * ys, weight * weight) + EPS)
        out = jnp.einsum('bsi,io->bso', Efou * ys[:, None, :], weight) * d[:, None, :]
        return out

    def _L0_ffn_ref(x, W_r, W_k, W_v, mu_r, mu_k):
        import jax, jax.numpy as jnp
        import numpy as np
        DIM = 512

        def _reference_tuple_inner(x, W_r, W_k, W_v, mu_r, mu_k):
            B, T, C = x.shape
            x_prev = jnp.concatenate([jnp.zeros((B, 1, C), x.dtype), x[:, :-1, :]], axis=1)
            xr = mu_r * x + (1.0 - mu_r) * x_prev
            xk = mu_k * x + (1.0 - mu_k) * x_prev
            r = jax.nn.sigmoid(jnp.einsum('btc,dc->btd', xr, W_r))
            k = jnp.einsum('btc,dc->btd', xk, W_k)
            k_act = jnp.square(jax.nn.relu(k))
            out = r * jnp.einsum('btc,dc->btd', k_act, W_v)
            new_state = x[:, -1, :]
            return (out, new_state)
        return _reference_tuple_inner(x, W_r, W_k, W_v, mu_r, mu_k)[0]
    x = x + _L0_attn_ref(_L0_cond_ref(cond_1024, x, L0_cond_W_z, L0_cond_U_z, L0_cond_C_z, L0_cond_b_z, L0_cond_W_r, L0_cond_U_r, L0_cond_C_r, L0_cond_b_r, L0_cond_W, L0_cond_U, L0_cond_C, L0_cond_b), L0_attn_W, L0_attn_bias)
    x = x + _L0_ffn_ref(_L0_cond2_ref(x, cond_1024, L0_cond2_weight), L0_ffn_W_r, L0_ffn_W_k, L0_ffn_W_v, L0_ffn_mu_r, L0_ffn_mu_k)
    return x

_drawn_inputs = setup_inputs


def setup_inputs(seed=0):
    import zlib

    import numpy as np

    out = dict(_drawn_inputs(seed))
    spreads = {'L0_cond_b_z': (0.0, 0.403), 'L0_cond_b_r': (0.0, 2.0), 'L0_cond_b': (0.0, 0.1)}
    factors = {'L0_cond_U_z': 4.671, 'L0_cond_W_r': 8.0, 'L0_cond_U_r': 38.584, 'L0_cond_C_r': 5.789}
    for name, (base, spread) in spreads.items():
        noise = np.random.default_rng([zlib.crc32(name.encode()), seed]).standard_normal(out[name].shape)
        drawn = base * np.exp(spread * noise) if base else spread * noise
        out[name] = jnp.asarray(drawn.astype(out[name].dtype))
    for name, factor in factors.items():
        out[name] = (out[name] * factor).astype(out[name].dtype)
    return out
```

```python
from contextlib import ExitStack

import numpy as np

import concourse.bass as bass
from concourse import mybir

F32 = mybir.dt.float32
F32R = mybir.dt.float32r
F16 = mybir.dt.float16
U32 = mybir.dt.uint32
ALU = mybir.AluOpType
ACT = mybir.ActivationFunctionType
AX_X = mybir.AxisListType.X
RMAX = bass.bass_isa.ReduceOp.max

P = 128
B, T, D = 64, 128, 512
KT = D // P
STEPS = 4
WINDOWS = T // STEPS
N = STEPS * B
HALF = KT // 2
STATE_SCALE = 2.0 ** 14
WEIGHT_TOP = 2.0 ** 14
TINY = 2.0 ** -90
EXPONENT = 0x7F800000
PASSES = ((0, 0), (0, 1), (1, 0))
EPS = 1e-08
YS_SCALE = float(np.float32(1.0) / np.sqrt(np.float32(D)))

W16 = ["attn", "u_r", "u_z", "u_h"]
W32 = ["cond", "key", "gate", "value", "w_r", "w_z", "w_h"]
WC = ["c_r", "c_z", "c_h"]
STAGED = WC + ["attn", "cond", "cond_sq", "u_r", "u_z", "u_h", "key", "gate", "value", "w_r", "w_z", "w_h"]
SLOTS = 3
B_R, B_Z, B_H, MU_R, MU_K = range(5)
NVEC = 5
PRODUCTS = ["attn", "hproj", "cond", "key", "gate", "value", "rproj", "zproj"]


def gru_ffn_kernel(nc, x, weights, small, bias_row, out):
    ctx = ExitStack()
    with ctx:
        def sb(name, shape, dt=F32):
            return ctx.enter_context(nc.sbuf_tensor(name, shape, dt))

        def sem(name):
            return ctx.enter_context(nc.semaphore(name))

        def psum(name, shape):
            return ctx.enter_context(nc.psum_tensor(name, shape, F32))

        wt = {n: sb("w_" + n, [P, 2, KT, D], F32R) for n in W32}
        wt |= {n: sb("w_" + n, [P, 2, KT, D], F16) for n in W16}
        x_parts = sb("x_parts", [P, 2, KT, N], F32R)
        a_parts = sb("a_parts", [P, 2, KT, N], F32R)
        b_parts = sb("b_parts", [P, 2, KT, N], F32R)
        hist = sb("hist", [P, 2, KT, STEPS, B], F16)
        rh_parts = sb("rh_parts", [P, 2, KT, B], F16)
        YW = (STEPS + 1) * B
        scratch = sb("scratch", [P, 5 * KT * N + KT * YW])
        bufs = scratch[:, 0:5 * KT * N].rearrange("p (i k n) -> p i k n", i=5, k=KT)
        rproj, zproj, hproj, x2, raw = (bufs[:, i] for i in range(5))
        yy = scratch[:, 5 * KT * N:5 * KT * N + KT * YW].rearrange("p (k n) -> p k n", k=KT)
        y_now = yy[:, :, B:YW]
        y_shift = yy[:, :, 0:N]
        stage = scratch[:, 0:SLOTS * KT * D].rearrange("p (i k m) -> p i k m", i=SLOTS, k=KT)
        work = sb("work", [P, 4 * KT * B])
        rg, zg, hc, state = (work[:, i * KT * B:(i + 1) * KT * B].rearrange("p (k b) -> p k b", k=KT)
                             for i in range(4))
        bias_in, bias_sum = work[0:1, 0:D], work[0:1, D:2 * D]
        cond_v = {n: sb("v_" + n, [P, KT, B]) for n in WC}
        ys = sb("ys", [P, KT, B])
        demod = sb("demod", [P, KT, B])
        vec = sb("vec", [P, NVEC, KT])
        rest = sb("rest", [P, NVEC, KT])
        attn_bias = sb("attn_bias", [P, KT])
        wmax = sb("wmax", [P, len(W16)])
        wtop = sb("wtop", [P, len(W16)])
        wpow = sb("wpow", [P, len(W16)])
        wrec = sb("wrec", [P, len(W16)])
        wscale = sb("wscale", [P, len(W16)])
        unscale = sb("unscale", [P, len(W16)])
        zero = sb("zero", [P, 1])
        one = sb("one", [P, 1])

        ps_r, ps_z, ps_c = (psum("ps_" + n, [P, 2, KT, B])[:, 0] for n in "rzc")
        ps_even = [psum(f"ps_even{h}", [P, HALF, N]) for h in range(2)]
        ps_odd = [psum(f"ps_odd{h}", [P, HALF, N]) for h in range(2)]

        small_in = sem("small_in")
        stage_in = [sem(f"stage_in{i}") for i in range(SLOTS)]
        consts_done, bias_done, bias_acc, bias_col = sem("consts_done"), sem("bias_done"), sem("bias_acc"), sem("bias_col")
        cgate_acc, cgate_taken = sem("cgate_acc"), sem("cgate_taken")
        scan_done, sq_done, demod_acc, demod_done = sem("scan_done"), sem("sq_done"), sem("demod_acc"), sem("demod_done")
        ysq_done, root_done = sem("ysq_done"), sem("root_done")
        max_done, top_done, pow_done, scale_done = sem("max_done"), sem("top_done"), sem("pow_done"), sem("scale_done")
        w_hi, w_lo = sem("w_hi"), sem("w_lo")
        cleared = sem("cleared")
        r_acc, z_acc, c_acc = sem("r_acc"), sem("z_acc"), sem("c_acc")
        acc = {n: sem(n + "_acc") for n in PRODUCTS}
        taken = {n: sem(n + "_taken") for n in PRODUCTS}
        r_pre, z_pre, c_pre = sem("r_pre"), sem("z_pre"), sem("c_pre")
        r_sig, z_sig, c_tanh = sem("r_sig"), sem("z_sig"), sem("c_tanh")
        rh_full, rh_hi, rh_ready = sem("rh_full"), sem("rh_hi"), sem("rh_ready")
        diff_done, zdiff_done, state_done = sem("diff_done"), sem("zdiff_done"), sem("state_done")
        h_hi, h_ready = sem("h_hi"), sem("h_ready")
        x_hi, x_ready = sem("x_hi"), sem("x_ready")
        x2_done, xs_done, xs_hi, xs_ready = sem("x2_done"), sem("xs_done"), sem("xs_hi"), sem("xs_ready")
        prev_k_tile, mix_k, xk_hi, xk_ready = sem("prev_k_tile"), sem("mix_k"), sem("xk_hi"), sem("xk_ready")
        prev_r_tile, mix_r, xr_hi, xr_ready = sem("prev_r_tile"), sem("mix_r"), sem("xr_hi"), sem("xr_ready")
        y_kept = sem("y_kept")
        relu_sq, kact_hi, kact_ready = sem("relu_sq"), sem("kact_hi"), sem("kact_ready")
        out_ready = sem("out_ready")
        raw_in = [sem(f"raw_in{h}") for h in range(2)]
        res_in = [sem(f"res_in{h}") for h in range(2)]
        out_stored = [sem(f"out_stored{h}") for h in range(2)]

        def wait(eng, semaphore, value):
            if not isinstance(value, int) or value > 0:
                eng.wait_ge(semaphore, value)

        def halves(g, h):
            return 2 * g + h + 1

        def half(buf, h):
            return buf[:, HALF * h:HALF * h + HALF]

        def over_time(a):
            k = a.shape[1]
            return a.unsqueeze(2).broadcast_to([P, k, STEPS, B])

        def by_time(a):
            return a.rearrange("p k (t b) -> p k t b", t=STEPS)

        def at_step(a, s):
            return a[:, :, s * B:(s + 1) * B]

        def slot(name):
            return STAGED.index(name) % SLOTS

        def staged(eng, name):
            i = STAGED.index(name)
            loads = sum(1 for n in STAGED[i % SLOTS:i + 1:SLOTS] if n != "cond_sq")
            eng.wait_ge(stage_in[i % SLOTS], 16 * loads)
            return stage[:, i % SLOTS]

        split_order = [n for n in STAGED if n in wt]

        def used_up(eng, name):
            if name in WC:
                eng.wait_ge(cgate_acc, WC.index(name) + 1)
            elif name == "cond_sq":
                eng.wait_ge(demod_acc, 1)
            else:
                eng.wait_ge(w_lo, split_order.index(name) + 1)

        block = ctx.enter_context(nc.Block())

        @block.sync
        def _(sp):
            sp.dma_start(vec[:, :, :], small[:, 0:NVEC * KT]).then_inc(small_in, 16)
            sp.dma_start(ys[:, :, :], small[:, NVEC * KT:NVEC * KT + KT * B]).then_inc(small_in, 16)
            sp.dma_start(bias_in, bias_row).then_inc(small_in, 16)
            for i, name in enumerate(STAGED):
                if name != "cond_sq":
                    if i >= SLOTS:
                        used_up(sp, STAGED[i - SLOTS])
                    sp.dma_start(stage[:, slot(name)], weights[name]).then_inc(stage_in[slot(name)], 16)

            def load_raw(g):
                for h in range(2):
                    sp.dma_start(half(raw, h), x[g][:, HALF * h:HALF * h + HALF]).then_inc(raw_in[h], 16)

            def window(g, gru=True, tail=True, proj=True):
                if proj:
                    if tail:
                        sp.wait_ge(kact_ready, halves(g - 1, 1))
                    else:
                        sp.wait_ge(x_ready, halves(g, 1))
                    load_raw(g + 1)
                if tail:
                    for h in range(2):
                        sp.wait_ge(out_ready, halves(g - 1, h))
                        sp.dma_start(out[g - 1][:, HALF * h:HALF * h + HALF], half(x2, h)).then_inc(out_stored[h], 16)
                if gru:
                    for h in range(2):
                        if tail:
                            sp.wait_ge(out_stored[h], 16 * g)
                        sp.dma_start(half(x2, h), x[g][:, HALF * h:HALF * h + HALF]).then_inc(res_in[h], 16)

            for name in STAGED[-SLOTS:]:
                used_up(sp, name)
            load_raw(0)
            window(0, tail=False)
            with sp.Fori(1, WINDOWS - 1) as g:
                window(g)
            window(WINDOWS - 1, proj=False)
            window(WINDOWS, gru=False, proj=False)
            for h in range(2):
                sp.wait_ge(out_stored[h], 16 * WINDOWS)

        @block.tensor
        def _(pe):
            def tile_product(ps_tile, w, data, m, ks, first, last, **group):
                for k in ks:
                    for i, (wp, dp) in enumerate(PASSES):
                        mm = pe.matmul(ps_tile, w[:, wp, k, m * P:(m + 1) * P], data(dp, k),
                                       start=first and k == ks[0] and i == 0,
                                       stop=last and k == ks[-1] and i == len(PASSES) - 1, **group)
                return mm

            def step_product(ps, w, data, done):
                for m in range(KT):
                    mm = tile_product(ps[:, m], wt[w], data, m, range(KT), True, True)
                mm.then_inc(done, 1)

            def reset_update(g, s):
                wait(pe, h_ready, STEPS * g + s)
                step_product(ps_r, "u_r", lambda dp, k: hist[:, dp, k, (s - 1) % STEPS], r_acc)
                step_product(ps_z, "u_z", lambda dp, k: hist[:, dp, k, (s - 1) % STEPS], z_acc)

            def candidate(g, s):
                pe.wait_ge(rh_ready, STEPS * g + s + 1)
                step_product(ps_c, "u_h", lambda dp, k: rh_parts[:, dp, k], c_acc)

            def by_rows(name, ps, w, data, m):
                mm = tile_product(ps[m // HALF][:, m % HALF], wt[w], data, m, range(KT), True, True)
                if m % HALF == HALF - 1:
                    mm.then_inc(acc[name], 1)

            def by_cols(name, ps, w, data, k):
                for m in range(KT):
                    mm = tile_product(ps[m // HALF][:, m % HALF], wt[w], data, m, [k],
                                      k == 0 and m % HALF == 0, k == KT - 1, skip_group_check=True)
                    if k == KT - 1 and m % HALF == HALF - 1:
                        mm.then_inc(acc[name], 1)

            def parts(buf):
                return lambda dp, k: buf[:, dp, k]

            def attn(g, ms, gru=True):
                for m in ms:
                    if m % HALF == 0:
                        if gru:
                            pe.wait_ge(taken["rproj"], halves(g, m // HALF))
                        else:
                            pe.wait_ge(taken["gate"], halves(g - 2, m // HALF))
                            wait(pe, h_ready, STEPS * g)
                    by_rows("attn", ps_even, "attn", lambda dp, k: hist[:, dp, k].rearrange("p t b -> p (t b)"), m)

            def hidden_proj(g, ms):
                for m in ms:
                    if m % HALF == 0:
                        wait(pe, taken["zproj"], halves(g, m // HALF))
                    by_rows("hproj", ps_odd, "w_h", parts(x_parts), m)

            def cond(g, ms):
                for m in ms:
                    if m == 0:
                        pe.wait_ge(xs_ready, halves(g - 1, 1))
                    if m % HALF == 0:
                        pe.wait_ge(taken["attn"], halves(g - 1, m // HALF))
                    by_rows("cond", ps_even, "cond", parts(a_parts), m)

            def key(g, ks, gru=True):
                for k in ks:
                    if k == 0:
                        if gru:
                            pe.wait_ge(taken["hproj"], halves(g, 1))
                        else:
                            pe.wait_ge(taken["value"], halves(g - 2, 1))
                    if k % HALF == 0:
                        pe.wait_ge(xk_ready, halves(g - 1, k // HALF))
                    by_cols("key", ps_odd, "key", parts(b_parts), k)

            def gate(g, ms):
                for m in ms:
                    if m == 0:
                        pe.wait_ge(xr_ready, halves(g - 1, 1))
                    if m % HALF == 0:
                        pe.wait_ge(taken["cond"], halves(g - 1, m // HALF))
                    by_rows("gate", ps_even, "gate", parts(x_parts), m)

            def value(g, ks):
                for k in ks:
                    if k == 0:
                        pe.wait_ge(taken["key"], halves(g - 1, 1))
                    if k % HALF == 0:
                        pe.wait_ge(kact_ready, halves(g - 1, k // HALF))
                    by_cols("value", ps_odd, "value", parts(a_parts), k)

            def reset_proj(g, ms, tail=True):
                for m in ms:
                    if m == 0:
                        pe.wait_ge(x_ready, halves(g + 1, 1))
                    if m % HALF == 0 and tail:
                        pe.wait_ge(taken["gate"], halves(g - 1, m // HALF))
                    if m % HALF == 0 and not tail:
                        wait(pe, taken["rproj"], halves(g, m // HALF))
                    by_rows("rproj", ps_even, "w_r", parts(x_parts), m)

            def update_proj(g, ms, tail=True):
                for m in ms:
                    if m % HALF == 0 and tail:
                        pe.wait_ge(taken["value"], halves(g - 1, m // HALF))
                    if m % HALF == 0 and not tail:
                        wait(pe, taken["hproj"], halves(g, m // HALF))
                    by_rows("zproj", ps_odd, "w_z", parts(x_parts), m)

            def window(g, gru=True, tail=True, proj=True):
                every = range(KT)
                if gru:
                    reset_update(g, 0)
                if tail:
                    attn(g, every, gru)
                if gru:
                    hidden_proj(g, every)
                    candidate(g, 0)
                if tail:
                    cond(g, every)
                if gru:
                    reset_update(g, 1)
                if tail:
                    key(g, range(0, 3), gru)
                if gru:
                    candidate(g, 1)
                if tail:
                    key(g, range(3, 4), gru)
                    gate(g, range(0, 2))
                if gru:
                    reset_update(g, 2)
                if tail:
                    gate(g, range(2, 4))
                    value(g, range(0, 1))
                if gru:
                    candidate(g, 2)
                if tail:
                    value(g, range(1, 4))
                if gru:
                    reset_update(g, 3)
                if proj:
                    reset_proj(g, every, tail)
                if gru:
                    candidate(g, 3)
                if proj:
                    update_proj(g, every, tail)

            pe.wait_ge(small_in, 48)
            for name, ps in zip(WC, (ps_r, ps_z, ps_c)):
                w = staged(pe, name)
                for m in range(KT):
                    for k in range(KT):
                        mm = pe.matmul(ps[:, m], w[:, k, m * P:(m + 1) * P], ys[:, k], start=k == 0, stop=k == KT - 1)
                mm.then_inc(cgate_acc, 1)
            pe.wait_ge(consts_done, 3)
            pe.wait_ge(bias_done, 1)
            for m in range(KT):
                mm = pe.matmul(ps_even[0][:, 0, m:m + 1], bias_sum[:, m * P:(m + 1) * P], one[0:1, :],
                               start=True, stop=True)
            mm.then_inc(bias_acc, 1)
            w = stage[:, slot("cond_sq")]
            pe.wait_ge(sq_done, 1)
            pe.wait_ge(ysq_done, 2)
            for m in range(KT):
                for k in range(KT):
                    mm = pe.matmul(ps_even[1][:, 0, m * B:(m + 1) * B], w[:, k, m * P:(m + 1) * P], rg[:, k],
                                   start=k == 0, stop=k == KT - 1)
            mm.then_inc(demod_acc, 1)
            pe.wait_ge(w_hi, len(split_order))
            pe.wait_ge(w_lo, len(split_order))
            pe.wait_ge(cgate_taken, len(WC))
            pe.wait_ge(cleared, 3)
            pe.wait_ge(x_ready, halves(0, 1))
            for m in range(KT):
                by_rows("rproj", ps_even, "w_r", parts(x_parts), m)
            for m in range(KT):
                by_rows("zproj", ps_odd, "w_z", parts(x_parts), m)
            window(0, tail=False)
            with pe.Fori(1, WINDOWS - 1) as g:
                window(g)
            window(WINDOWS - 1, proj=False)
            window(WINDOWS, gru=False, proj=False)

        @block.scalar
        def _(act):
            def sigmoid(buf, pre, done, n):
                act.wait_ge(pre, n)
                act.activation(buf, buf, ACT.Sigmoid).then_inc(done, 1)

            def gates(g, s):
                n = STEPS * g + s + 1
                sigmoid(rg, r_pre, r_sig, n)
                sigmoid(zg, z_pre, z_sig, n)

            def tanh(g, s):
                n = STEPS * g + s + 1
                act.wait_ge(c_pre, n)
                act.activation(hc, hc, ACT.Tanh).then_inc(c_tanh, 1)

            def take_attn(q, h):
                if h == 0:
                    wait(act, out_ready, halves(q - 1, 1))
                act.wait_ge(acc["attn"], halves(q, h))
                for m in range(HALF):
                    a = act.activation(y_now[:, HALF * h + m], ps_even[h][:, m], ACT.Identity,
                                       bias=attn_bias[:, HALF * h + m:HALF * h + m + 1],
                                       scale=unscale[:, W16.index("attn"):W16.index("attn") + 1])
                a.then_inc(taken["attn"], 1)

            def split_hi(dst, src, ready, done, q, h):
                act.wait_ge(ready, halves(q, h))
                act.copy(half(dst[:, 0], h), half(src, h)).then_inc(done, 1)

            def prev(q, h, mu, done, last_reader):
                wait(act, last_reader, halves(q, h))
                if last_reader is x_ready:
                    act.wait_ge(taken["cond"], halves(q, h))
                for m in range(HALF * h, HALF * h + HALF):
                    act.mul(raw[:, m], y_shift[:, m], rest[:, mu, m:m + 1]).then_inc(done, 1)

            def keep_last(q):
                act.wait_ge(prev_r_tile, KT * (q + 1))
                act.copy(yy[:, :, 0:B], yy[:, :, N:YW]).then_inc(y_kept, 1)

            def relu(q, h):
                act.wait_ge(acc["key"], halves(q, h))
                act.wait_ge(xr_ready, halves(q, h))
                act.activation(half(raw, h), ps_odd[h][:, :, :], ACT.Relu).then_inc(taken["key"], 1)

            def take_gate(q, h):
                act.wait_ge(y_kept, q + 1)
                act.wait_ge(acc["gate"], halves(q, h))
                act.activation(half(y_now, h), ps_even[h][:, :, :], ACT.Sigmoid).then_inc(taken["gate"], 1)

            def split_x(g, h, tail=True):
                act.wait_ge(raw_in[h], 16 * (g + 1))
                if tail:
                    act.wait_ge(acc["gate"], halves(g - 2, 1))
                elif g > 0:
                    act.wait_ge(acc["hproj"], halves(g - 1, 1))
                act.copy(half(x_parts[:, 0], h), half(raw, h)).then_inc(x_hi, 1)

            def window(g, gru=True, tail=True, proj=True):
                q = g - 1
                if gru:
                    gates(g, 0)
                if tail:
                    take_attn(q, 0)
                    take_attn(q, 1)
                    split_hi(a_parts, y_now, xs_done, xs_hi, q, 0)
                    split_hi(a_parts, y_now, xs_done, xs_hi, q, 1)
                if gru:
                    tanh(g, 0)
                if tail:
                    for h in range(2):
                        prev(q, h, MU_K, prev_k_tile, x_ready)
                        split_hi(b_parts, raw, mix_k, xk_hi, q, h)
                if gru:
                    gates(g, 1)
                if tail:
                    for h in range(2):
                        prev(q, h, MU_R, prev_r_tile, xk_ready)
                    for h in range(2):
                        split_hi(x_parts, raw, mix_r, xr_hi, q, h)
                    keep_last(q)
                if gru:
                    tanh(g, 1)
                if tail:
                    relu(q, 0)
                    relu(q, 1)
                    split_hi(a_parts, raw, relu_sq, kact_hi, q, 0)
                    split_hi(a_parts, raw, relu_sq, kact_hi, q, 1)
                if gru:
                    gates(g, 2)
                if tail:
                    take_gate(q, 0)
                    take_gate(q, 1)
                if gru:
                    tanh(g, 2)
                if proj:
                    split_x(g + 1, 0, tail)
                    split_x(g + 1, 1, tail)
                if gru:
                    gates(g, 3)
                    tanh(g, 3)

            act.wait_ge(small_in, 48)
            for i, (name, ps, b) in enumerate(zip(WC, (ps_r, ps_z, ps_c), (B_R, B_Z, B_H))):
                act.wait_ge(cgate_acc, i + 1)
                for m in range(KT):
                    a = act.activation(cond_v[name][:, m], ps[:, m], ACT.Identity, bias=vec[:, b, m:m + 1])
                a.then_inc(cgate_taken, 1)
            act.wait_ge(bias_acc, 1)
            act.copy(attn_bias[:, :], ps_even[0][:, 0, 0:KT]).then_inc(bias_col, 1)
            for name in split_order:
                w = staged(act, name)
                if name in W16:
                    i = W16.index(name)
                    act.wait_ge(scale_done, 2 * i + 1)
                    act.mul(wt[name][:, 0], w, wscale[:, i:i + 1]).then_inc(w_hi, 1)
                else:
                    act.copy(wt[name][:, 0], w).then_inc(w_hi, 1)
                if name == "u_r":
                    act.wait_ge(demod_done, 1)
                    act.activation(hc, zg, ACT.Sqrt).then_inc(root_done, 1)
            split_x(0, 0, tail=False)
            split_x(0, 1, tail=False)
            window(0, tail=False)
            with act.Fori(1, WINDOWS - 1) as g:
                window(g)
            window(WINDOWS - 1, proj=False)
            window(WINDOWS, gru=False, proj=False)

        @block.gpsimd
        def _(pool):
            for i in range(len(W16)):
                pool.wait_ge(max_done, i + 1)
                pool.partition_all_reduce(wtop[:, i:i + 1], wmax[:, i:i + 1], P, RMAX).then_inc(top_done, 1)

            def square(q, h):
                pool.wait_ge(taken["key"], halves(q, h))
                pool.tensor_tensor(half(raw, h), half(raw, h), half(raw, h), ALU.mult).then_inc(relu_sq, 1)

            def residual(q, h):
                pool.wait_ge(taken["value"], halves(q, h))
                pool.tensor_tensor(half(x2, h), half(x2, h), half(y_now, h), ALU.add).then_inc(out_ready, 1)

            def window(g):
                for stage_of in (square, residual):
                    for h in range(2):
                        stage_of(g - 1, h)

            with pool.Fori(1, WINDOWS + 1) as g:
                window(g)

        @block.vector
        def _(dve):
            def add_projection(dst, ps, w, name, proj, g, s, acc_sem, done):
                if s == 0:
                    dve.wait_ge(taken[name], halves(g, 1))
                dve.wait_ge(acc_sem, STEPS * g + s + 1)
                i = W16.index(w)
                dve.scalar_tensor_tensor(dst, ps, unscale[:, i:i + 1], at_step(proj, s), ALU.mult, ALU.add).then_inc(done, 1)

            def reset(g, s):
                n = STEPS * g + s + 1
                add_projection(rg, ps_r, "u_r", "rproj", rproj, g, s, r_acc, r_pre)
                dve.wait_ge(r_sig, n)
                dve.tensor_tensor(rg, rg, state, ALU.mult).then_inc(rh_full, 1)
                dve.wait_ge(rh_full, n)
                dve.tensor_copy(rh_parts[:, 0], rg).then_inc(rh_hi, 1)
                dve.wait_ge(rh_hi, n)
                dve.tensor_tensor(rh_parts[:, 1], rg, rh_parts[:, 0], ALU.subtract).then_inc(rh_ready, 1)

            def update(g, s):
                add_projection(zg, ps_z, "u_z", "zproj", zproj, g, s, z_acc, z_pre)

            def new_state(g, s):
                n = STEPS * g + s + 1
                add_projection(hc, ps_c, "u_h", "hproj", hproj, g, s, c_acc, c_pre)
                dve.wait_ge(c_tanh, n)
                dve.scalar_tensor_tensor(hc, hc, STATE_SCALE, state, ALU.mult, ALU.subtract).then_inc(diff_done, 1)
                dve.wait_ge(diff_done, n)
                dve.wait_ge(z_sig, n)
                dve.tensor_tensor(hc, hc, zg, ALU.mult).then_inc(zdiff_done, 1)
                dve.wait_ge(zdiff_done, n)
                dve.tensor_tensor(state, state, hc, ALU.add).then_inc(state_done, 1)
                dve.wait_ge(state_done, n)
                dve.tensor_copy(hist[:, 0, :, s], state).then_inc(h_hi, 1)
                dve.wait_ge(h_hi, n)
                dve.tensor_tensor(hist[:, 1, :, s], state, hist[:, 0, :, s], ALU.subtract).then_inc(h_ready, 1)

            def take_proj(name, g, h, dst, ps, v):
                dve.wait_ge(acc[name], halves(g, h))
                dve.tensor_tensor(by_time(half(dst, h)), by_time(ps[h]), over_time(half(cond_v[v], h)), ALU.add)\
                    .then_inc(taken[name], 1)

            def take_rproj(g, h):
                take_proj("rproj", g, h, rproj, ps_even, "c_r")

            def take_zproj(g, h):
                take_proj("zproj", g, h, zproj, ps_odd, "c_z")

            def take_hproj(g, h):
                take_proj("hproj", g, h, hproj, ps_odd, "c_h")

            def split_lo(dst, src, hi, done, q, h):
                dve.wait_ge(hi, halves(q, h))
                dve.tensor_tensor(half(dst[:, 1], h), half(src, h), half(dst[:, 0], h).bitcast(F32), ALU.subtract)\
                    .then_inc(done, 1)

            def style(q, h):
                dve.wait_ge(taken["attn"], halves(q, h))
                dve.wait_ge(res_in[h], 16 * (q + 1))
                dve.tensor_tensor(half(x2, h), half(x2, h), half(y_now, h), ALU.add).then_inc(x2_done, 1)
                dve.wait_ge(x2_done, halves(q, h))
                dve.tensor_tensor(by_time(half(y_now, h)), by_time(half(x2, h)), over_time(half(ys, h)), ALU.mult)\
                    .then_inc(xs_done, 1)

            def take_cond(q, h):
                dve.wait_ge(acc["cond"], halves(q, h))
                dve.tensor_tensor(by_time(half(y_now, h)), by_time(ps_even[h]), over_time(half(demod, h)), ALU.mult)\
                    .then_inc(taken["cond"], 1)

            def mix(q, h, mu, prev_tile, done):
                dve.wait_ge(taken["cond"], halves(q, h))
                for m in range(HALF * h, HALF * h + HALF):
                    dve.wait_ge(prev_tile, KT * q + m + 1)
                    d = dve.scalar_tensor_tensor(raw[:, m], y_now[:, m], vec[:, mu, m:m + 1], raw[:, m],
                                                 ALU.mult, ALU.add)
                d.then_inc(done, 1)

            def take_value(q, h):
                dve.wait_ge(acc["value"], halves(q, h))
                dve.wait_ge(taken["gate"], halves(q, h))
                dve.tensor_tensor(half(y_now, h), half(y_now, h), ps_odd[h][:, :, :], ALU.mult)\
                    .then_inc(taken["value"], 1)

            def window(g, gru=True, tail=True, proj=True):
                q = g - 1
                if gru:
                    reset(g, 0)
                    update(g, 0)
                if tail:
                    style(q, 0)
                    style(q, 1)
                    split_lo(a_parts, y_now, xs_hi, xs_ready, q, 0)
                    split_lo(a_parts, y_now, xs_hi, xs_ready, q, 1)
                if gru:
                    take_hproj(g, 0)
                    take_hproj(g, 1)
                    new_state(g, 0)
                if tail:
                    for h in range(2):
                        take_cond(q, h)
                        mix(q, h, MU_K, prev_k_tile, mix_k)
                        split_lo(b_parts, raw, xk_hi, xk_ready, q, h)
                if gru:
                    reset(g, 1)
                    update(g, 1)
                if tail:
                    for h in range(2):
                        mix(q, h, MU_R, prev_r_tile, mix_r)
                    for h in range(2):
                        split_lo(x_parts, raw, xr_hi, xr_ready, q, h)
                if gru:
                    new_state(g, 1)
                if tail:
                    for h in range(2):
                        split_lo(a_parts, raw, kact_hi, kact_ready, q, h)
                if gru:
                    reset(g, 2)
                    update(g, 2)
                    new_state(g, 2)
                if proj:
                    split_lo(x_parts, raw, x_hi, x_ready, g + 1, 0)
                    split_lo(x_parts, raw, x_hi, x_ready, g + 1, 1)
                if tail:
                    take_value(q, 0)
                    take_value(q, 1)
                if gru:
                    reset(g, 3)
                    update(g, 3)
                if proj:
                    take_rproj(g + 1, 0)
                    take_rproj(g + 1, 1)
                if gru:
                    new_state(g, 3)
                if proj:
                    take_zproj(g + 1, 0)
                    take_zproj(g + 1, 1)

            dve.memset(zero[:, :], 0.0).then_inc(consts_done, 1)
            dve.memset(one[:, :], 1.0).then_inc(consts_done, 1)
            dve.wait_ge(small_in, 48)
            dve.tensor_scalar(rest[:, :, :], vec[:, :, :], -1.0, 1.0, ALU.mult, ALU.add).then_inc(consts_done, 1)
            dve.wait_ge(consts_done, 1)
            dve.tensor_tensor_scan(bias_sum, zero[0:1, :].broadcast_to([1, D]), bias_in, 0.0, ALU.add, ALU.add)\
                .then_inc(bias_done, 1)
            for name in split_order:
                w = staged(dve, name)
                i_split = split_order.index(name)
                if name == "attn":
                    for k in range(KT):
                        d = dve.tensor_tensor_scan(w[:, k], zero[:, :].broadcast_to([P, D]), w[:, k], 0.0, ALU.add, ALU.add)
                    d.then_inc(scan_done, 1)
                    dve.wait_ge(scan_done, 1)
                if name in W16:
                    i = W16.index(name)
                    dve.tensor_reduce(wmax[:, i:i + 1], w.rearrange("p k m -> p (k m)"), AX_X, ALU.max,
                                      apply_absolute_value=True).then_inc(max_done, 1)
                    dve.wait_ge(top_done, i + 1)
                    dve.tensor_scalar(wtop[:, i:i + 1], wtop[:, i:i + 1], TINY, None, ALU.max).then_inc(pow_done, 1)
                    dve.wait_ge(pow_done, 3 * i + 1)
                    dve.tensor_scalar(wpow[:, i:i + 1].bitcast(U32), wtop[:, i:i + 1].bitcast(U32), EXPONENT, None,
                                      ALU.bitwise_and).then_inc(pow_done, 1)
                    dve.wait_ge(pow_done, 3 * i + 2)
                    dve.reciprocal(wrec[:, i:i + 1], wpow[:, i:i + 1]).then_inc(pow_done, 1)
                    dve.wait_ge(pow_done, 3 * i + 3)
                    dve.tensor_scalar(wscale[:, i:i + 1], wrec[:, i:i + 1], WEIGHT_TOP, None, ALU.mult).then_inc(scale_done, 1)
                    dve.tensor_scalar(unscale[:, i:i + 1], wpow[:, i:i + 1], 1.0 / (WEIGHT_TOP * STATE_SCALE), None,
                                      ALU.mult).then_inc(scale_done, 1)
                    dve.wait_ge(scale_done, 2 * i + 2)
                    dve.wait_ge(w_hi, i_split + 1)
                    dve.scalar_tensor_tensor(wt[name][:, 1].rearrange("p k m -> p (k m)"),
                                             w.rearrange("p k m -> p (k m)"), wscale[:, i:i + 1],
                                             wt[name][:, 0].rearrange("p k m -> p (k m)"), ALU.mult, ALU.subtract)\
                        .then_inc(w_lo, 1)
                else:
                    if name == "cond":
                        used_up(dve, STAGED[STAGED.index("cond_sq") - SLOTS])
                        dve.tensor_tensor(stage[:, slot("cond_sq")], w, w, ALU.mult).then_inc(sq_done, 1)
                        dve.wait_ge(cgate_acc, len(WC))
                        dve.wait_ge(bias_acc, 1)
                        dve.tensor_scalar(ys[:, :, :], ys[:, :, :], YS_SCALE, None, ALU.mult).then_inc(ysq_done, 1)
                        dve.wait_ge(ysq_done, 1)
                        dve.tensor_tensor(rg, ys[:, :, :], ys[:, :, :], ALU.mult).then_inc(ysq_done, 1)
                    dve.wait_ge(w_hi, i_split + 1)
                    dve.tensor_tensor(wt[name][:, 1], w, wt[name][:, 0].bitcast(F32), ALU.subtract).then_inc(w_lo, 1)
                if name == "u_r":
                    dve.wait_ge(demod_acc, 1)
                    dve.tensor_scalar(zg, ps_even[1][:, 0].rearrange("p (k b) -> p k b", k=KT), EPS, None, ALU.add)\
                        .then_inc(demod_done, 1)
                    dve.wait_ge(root_done, 1)
                    dve.reciprocal(state, hc).then_inc(demod_done, 1)
                    dve.wait_ge(demod_done, 2)
                    dve.tensor_tensor(hc, state, state, ALU.mult).then_inc(demod_done, 1)
                    dve.wait_ge(demod_done, 3)
                    dve.tensor_tensor(hc, hc, zg, ALU.mult).then_inc(demod_done, 1)
                    dve.wait_ge(demod_done, 4)
                    dve.tensor_scalar(hc, hc, -0.5, 1.5, ALU.mult, ALU.add).then_inc(demod_done, 1)
                    dve.wait_ge(demod_done, 5)
                    dve.tensor_tensor(demod[:, :, :], state, hc, ALU.mult).then_inc(demod_done, 1)
                    dve.wait_ge(demod_done, 6)
            dve.wait_ge(w_lo, len(split_order))
            dve.memset(state, 0.0).then_inc(cleared, 1)
            dve.memset(hist[:, :, :, STEPS - 1], 0.0).then_inc(cleared, 1)
            dve.memset(yy[:, :, 0:B], 0.0).then_inc(cleared, 1)
            dve.wait_ge(cleared, 3)
            split_lo(x_parts, raw, x_hi, x_ready, 0, 0)
            split_lo(x_parts, raw, x_hi, x_ready, 0, 1)
            take_rproj(0, 0)
            take_rproj(0, 1)
            take_zproj(0, 0)
            take_zproj(0, 1)
            window(0, tail=False)
            with dve.Fori(1, WINDOWS - 1) as g:
                window(g)
            window(WINDOWS - 1, proj=False)
            window(WINDOWS, gru=False, proj=False)


def kernel(**inputs):
    import concourse.bacc as bacc
    from concourse.bass_utils import run_bass_kernel_spmd as run

    f32 = {n: np.ascontiguousarray(a) for n, a in inputs.items()}

    def weight(name, turned=False):
        a = f32[name].T if turned else f32[name]
        return np.ascontiguousarray(a.reshape(KT, P, D).transpose(1, 0, 2))

    def columns(a):
        return a.reshape(KT, P, -1).transpose(1, 0, 2).reshape(P, -1)

    arrays = {
        "x": np.ascontiguousarray(f32["x"].reshape(B, WINDOWS, STEPS, KT, P).transpose(1, 4, 3, 2, 0).reshape(WINDOWS, P, KT, N)),
        "small": np.ascontiguousarray(np.concatenate(
            [columns(f32[n]) for n in ("L0_cond_b_r", "L0_cond_b_z", "L0_cond_b", "L0_ffn_mu_r", "L0_ffn_mu_k")]
            + [columns(f32["cond_1024"].T)], axis=1)),
        "bias_row": f32["L0_attn_bias"].reshape(1, D),
    }
    sources = {
        "c_r": ("L0_cond_C_r",), "c_z": ("L0_cond_C_z",), "c_h": ("L0_cond_C",),
        "u_r": ("L0_cond_U_r",), "u_z": ("L0_cond_U_z",), "u_h": ("L0_cond_U",),
        "w_r": ("L0_cond_W_r",), "w_z": ("L0_cond_W_z",), "w_h": ("L0_cond_W",),
        "cond": ("L0_cond2_weight",), "attn": ("L0_attn_W", True),
        "key": ("L0_ffn_W_k", True), "gate": ("L0_ffn_W_r", True), "value": ("L0_ffn_W_v", True),
    }
    for name, source in sources.items():
        arrays["raw_" + name] = weight(*source)

    nc = bacc.Bacc("TRN2", target_bir_lowering=False, num_devices=1)
    dram = {n: nc.dram_tensor(n, a.shape, F32, kind="ExternalInput").ap() for n, a in arrays.items()}
    out = nc.dram_tensor("out", (WINDOWS, P, KT, N), F32, kind="ExternalOutput").ap()
    gru_ffn_kernel(nc, dram["x"], {n: dram["raw_" + n] for n in sources}, dram["small"], dram["bias_row"], out)
    r = run(nc, [arrays], core_ids=[0])
    y = np.asarray(r.results[0]["out"]).reshape(WINDOWS, P, KT, STEPS, B)
    return np.ascontiguousarray(y.transpose(4, 0, 3, 2, 1)).reshape(B, T, D)
```

```python
from contextlib import ExitStack

import numpy as np

import concourse.bass as bass
from concourse import mybir

F32 = mybir.dt.float32
F32R = mybir.dt.float32r
F16 = mybir.dt.float16
U32 = mybir.dt.uint32
ALU = mybir.AluOpType
ACT = mybir.ActivationFunctionType
AX_X = mybir.AxisListType.X
RMAX = bass.bass_isa.ReduceOp.max

P = 128
B, T, D = 64, 128, 512
KT = D // P
STEPS = 4
WINDOWS = T // STEPS
N = STEPS * B
HALF = KT // 2
STATE_SCALE = 2.0 ** 14
WEIGHT_TOP = 2.0 ** 14
TINY = 2.0 ** -90
EXPONENT = 0x7F800000
PASSES = ((0, 0), (0, 1), (1, 0))
EPS = 1e-08
YS_SCALE = float(np.float32(1.0) / np.sqrt(np.float32(D)))

W16 = ["attn", "u_r", "u_z", "u_h"]
W32 = ["cond", "key", "gate", "value", "w_r", "w_z", "w_h"]
WC = ["c_r", "c_z", "c_h"]
SLOT_OF = {"w_r": 0, "u_r": 1, "c_r": 2, "w_z": 3, "u_z": 2, "c_z": 0, "w_h": 1, "u_h": 3, "c_h": 0,
           "attn": 2, "cond": 3, "cond_sq": 4, "key": 2, "gate": 3, "value": 2}
SPLIT_ORDER = ["w_r", "u_r", "w_z", "u_z", "w_h", "u_h", "attn", "cond", "key", "gate", "value"]
MAX_ORDER = [n for n in SPLIT_ORDER if n in W16]
B_R, B_Z, B_H, MU_R, MU_K = range(5)
NVEC = 5
PRODUCTS = ["attn", "hproj", "cond", "key", "gate", "value", "rproj", "zproj"]


def gru_ffn_kernel(nc, x, weights, small, bias_row, out):
    ctx = ExitStack()
    with ctx:
        def sb(name, shape, dt=F32):
            return ctx.enter_context(nc.sbuf_tensor(name, shape, dt))

        def sem(name):
            return ctx.enter_context(nc.semaphore(name))

        def psum(name, shape):
            return ctx.enter_context(nc.psum_tensor(name, shape, F32))

        wt = {n: sb("w_" + n, [P, 2, KT, D], F32R) for n in W32}
        wt |= {n: sb("w_" + n, [P, 2, KT, D], F16) for n in W16}
        x_parts = sb("x_parts", [P, 2, KT, N], F32R)
        with nc.sbuf_tensor("stage_ab", [P, 2, KT, D], F32) as stage_ab:
            pass
        a_parts = sb("a_parts", [P, 2, KT, N], F32R)
        b_parts = sb("b_parts", [P, 2, KT, N], F32R)
        hist = sb("hist", [P, 2, KT, STEPS, B], F16)
        rh_parts = sb("rh_parts", [P, 2, KT, B], F16)
        YW = (STEPS + 1) * B
        scratch = sb("scratch", [P, 5 * KT * N + KT * YW])
        bufs = scratch[:, 0:5 * KT * N].rearrange("p (i k n) -> p i k n", i=5, k=KT)
        rproj, zproj, hproj, x2, raw = (bufs[:, i] for i in range(5))
        yy = scratch[:, 5 * KT * N:5 * KT * N + KT * YW].rearrange("p (k n) -> p k n", k=KT)
        y_now = yy[:, :, B:YW]
        y_shift = yy[:, :, 0:N]
        def rows(first):
            return scratch[:, first * KT * N:first * KT * N + KT * D].rearrange("p (k m) -> p k m", k=KT)
        slots = [rows(0), rows(2), stage_ab[:, 0], stage_ab[:, 1], rows(3)]
        ysq, dvar, droot, dinv, dtmp = (
            scratch[:, 5 * KT * N + i * KT * B:5 * KT * N + (i + 1) * KT * B].rearrange("p (k b) -> p k b", k=KT)
            for i in range(5))
        work = sb("work", [P, 4 * KT * B])
        rg, zg, hc, state = (work[:, i * KT * B:(i + 1) * KT * B].rearrange("p (k b) -> p k b", k=KT)
                             for i in range(4))
        bias_in, bias_sum = work[0:1, 0:D], work[0:1, D:2 * D]
        cond_v = {n: sb("v_" + n, [P, KT, B]) for n in WC}
        ys = sb("ys", [P, KT, B])
        demod = sb("demod", [P, KT, B])
        vec = sb("vec", [P, NVEC, KT])
        rest = sb("rest", [P, NVEC, KT])
        attn_bias = sb("attn_bias", [P, KT])
        wmax = sb("wmax", [P, len(W16)])
        wtop = sb("wtop", [P, len(W16)])
        wpow = sb("wpow", [P, len(W16)])
        wrec = sb("wrec", [P, len(W16)])
        wscale = sb("wscale", [P, len(W16)])
        unscale = sb("unscale", [P, len(W16)])
        zero = sb("zero", [P, 1])
        one = sb("one", [P, 1])

        ps_r, ps_z, ps_c = (psum("ps_" + n, [P, 2, KT, B])[:, 0] for n in "rzc")
        ps_even = [psum(f"ps_even{h}", [P, HALF, N]) for h in range(2)]
        ps_odd = [psum(f"ps_odd{h}", [P, HALF, N]) for h in range(2)]

        small_in = sem("small_in")
        stage_in = [sem(f"stage_in{i}") for i in range(max(SLOT_OF.values()))]
        consts_done, bias_done, bias_acc, bias_col = sem("consts_done"), sem("bias_done"), sem("bias_acc"), sem("bias_col")
        cgate_acc, cgate_taken = sem("cgate_acc"), sem("cgate_taken")
        scan_done, sq_done, demod_acc, demod_done = sem("scan_done"), sem("sq_done"), sem("demod_acc"), sem("demod_done")
        ysq_done, root_done = sem("ysq_done"), sem("root_done")
        max_done, top_done, pow_done, scale_done = sem("max_done"), sem("top_done"), sem("pow_done"), sem("scale_done")
        w_hi, w_lo = sem("w_hi"), sem("w_lo")
        cleared = sem("cleared")
        r_acc, z_acc, c_acc = sem("r_acc"), sem("z_acc"), sem("c_acc")
        acc = {n: sem(n + "_acc") for n in PRODUCTS}
        taken = {n: sem(n + "_taken") for n in PRODUCTS}
        r_pre, z_pre, c_pre = sem("r_pre"), sem("z_pre"), sem("c_pre")
        r_sig, z_sig, c_tanh = sem("r_sig"), sem("z_sig"), sem("c_tanh")
        rh_full, rh_hi, rh_ready = sem("rh_full"), sem("rh_hi"), sem("rh_ready")
        diff_done, zdiff_done, state_done = sem("diff_done"), sem("zdiff_done"), sem("state_done")
        h_hi, h_ready = sem("h_hi"), sem("h_ready")
        x_hi, x_ready = sem("x_hi"), sem("x_ready")
        x2_done, xs_done, xs_hi, xs_ready = sem("x2_done"), sem("xs_done"), sem("xs_hi"), sem("xs_ready")
        prev_k_tile, mix_k, xk_hi, xk_ready = sem("prev_k_tile"), sem("mix_k"), sem("xk_hi"), sem("xk_ready")
        prev_r_tile, mix_r, xr_hi, xr_ready = sem("prev_r_tile"), sem("mix_r"), sem("xr_hi"), sem("xr_ready")
        y_kept = sem("y_kept")
        relu_sq, kact_hi, kact_ready = sem("relu_sq"), sem("kact_hi"), sem("kact_ready")
        out_ready = sem("out_ready")
        raw_in = [sem(f"raw_in{h}") for h in range(2)]
        res_in = [sem(f"res_in{h}") for h in range(2)]
        out_stored = [sem(f"out_stored{h}") for h in range(2)]

        def wait(eng, semaphore, value):
            if not isinstance(value, int) or value > 0:
                eng.wait_ge(semaphore, value)

        def halves(g, h):
            return 2 * g + h + 1

        def half(buf, h):
            return buf[:, HALF * h:HALF * h + HALF]

        def over_time(a):
            k = a.shape[1]
            return a.unsqueeze(2).broadcast_to([P, k, STEPS, B])

        def by_time(a):
            return a.rearrange("p k (t b) -> p k t b", t=STEPS)

        def at_step(a, s):
            return a[:, :, s * B:(s + 1) * B]

        def occupants(name):
            names = list(SLOT_OF)
            return [n for n in names[:names.index(name)] if SLOT_OF[n] == SLOT_OF[name]]

        def staged(eng, name):
            eng.wait_ge(stage_in[SLOT_OF[name]], 16 * (len(occupants(name)) + 1))
            return slots[SLOT_OF[name]]

        def used_up(eng, name):
            if name in WC:
                eng.wait_ge(cgate_acc, WC.index(name) + 1)
            elif name == "cond_sq":
                eng.wait_ge(demod_acc, 1)
            else:
                eng.wait_ge(w_lo, SPLIT_ORDER.index(name) + 1)

        def weights_split(eng, name):
            eng.wait_ge(w_hi, SPLIT_ORDER.index(name) + 1)
            eng.wait_ge(w_lo, SPLIT_ORDER.index(name) + 1)

        block = ctx.enter_context(nc.Block())

        @block.sync
        def _(sp):
            def load_raw(g):
                for h in range(2):
                    sp.dma_start(half(raw, h), x[g][:, HALF * h:HALF * h + HALF]).then_inc(raw_in[h], 16)

            def load_res(g):
                for h in range(2):
                    wait(sp, out_stored[h], 16 * g)
                    sp.dma_start(half(x2, h), x[g][:, HALF * h:HALF * h + HALF]).then_inc(res_in[h], 16)

            sp.dma_start(vec[:, :, :], small[:, 0:NVEC * KT]).then_inc(small_in, 16)
            sp.dma_start(ys[:, :, :], small[:, NVEC * KT:NVEC * KT + KT * B]).then_inc(small_in, 16)
            sp.dma_start(bias_in, bias_row).then_inc(small_in, 16)
            load_raw(0)
            for name in weights:
                if name == "value":
                    used_up(sp, "cond_sq")
                    load_res(0)
                    load_raw(1)
                if occupants(name):
                    used_up(sp, occupants(name)[-1])
                sp.dma_start(slots[SLOT_OF[name]], weights[name]).then_inc(stage_in[SLOT_OF[name]], 16)

            def window(g, gru=True, proj=True):
                if proj:
                    sp.wait_ge(kact_ready, halves(g - 1, 1))
                    load_raw(g + 1)
                for h in range(2):
                    sp.wait_ge(out_ready, halves(g - 1, h))
                    sp.dma_start(out[g - 1][:, HALF * h:HALF * h + HALF], half(x2, h)).then_inc(out_stored[h], 16)
                if gru:
                    load_res(g)

            with sp.Fori(1, WINDOWS - 1) as g:
                window(g)
            window(WINDOWS - 1, proj=False)
            window(WINDOWS, gru=False, proj=False)
            for h in range(2):
                sp.wait_ge(out_stored[h], 16 * WINDOWS)

        @block.tensor
        def _(pe):
            def tile_product(ps_tile, w, data, m, ks, first, last, **group):
                for k in ks:
                    for i, (wp, dp) in enumerate(PASSES):
                        mm = pe.matmul(ps_tile, w[:, wp, k, m * P:(m + 1) * P], data(dp, k),
                                       start=first and k == ks[0] and i == 0,
                                       stop=last and k == ks[-1] and i == len(PASSES) - 1, **group)
                return mm

            def step_product(ps, w, data, done):
                for m in range(KT):
                    mm = tile_product(ps[:, m], wt[w], data, m, range(KT), True, True)
                mm.then_inc(done, 1)

            def reset_update(g, s):
                wait(pe, h_ready, STEPS * g + s)
                step_product(ps_r, "u_r", lambda dp, k: hist[:, dp, k, (s - 1) % STEPS], r_acc)
                step_product(ps_z, "u_z", lambda dp, k: hist[:, dp, k, (s - 1) % STEPS], z_acc)

            def candidate(g, s):
                pe.wait_ge(rh_ready, STEPS * g + s + 1)
                step_product(ps_c, "u_h", lambda dp, k: rh_parts[:, dp, k], c_acc)

            def by_rows(name, ps, w, data, m):
                mm = tile_product(ps[m // HALF][:, m % HALF], wt[w], data, m, range(KT), True, True)
                if m % HALF == HALF - 1:
                    mm.then_inc(acc[name], 1)

            def by_cols(name, ps, w, data, k):
                for m in range(KT):
                    mm = tile_product(ps[m // HALF][:, m % HALF], wt[w], data, m, [k],
                                      k == 0 and m % HALF == 0, k == KT - 1, skip_group_check=True)
                    if k == KT - 1 and m % HALF == HALF - 1:
                        mm.then_inc(acc[name], 1)

            def parts(buf):
                return lambda dp, k: buf[:, dp, k]

            def attn(g, ms, gru=True):
                for m in ms:
                    if m % HALF == 0:
                        if gru:
                            pe.wait_ge(taken["rproj"], halves(g, m // HALF))
                        else:
                            pe.wait_ge(taken["gate"], halves(g - 2, m // HALF))
                            wait(pe, h_ready, STEPS * g)
                    by_rows("attn", ps_even, "attn", lambda dp, k: hist[:, dp, k].rearrange("p t b -> p (t b)"), m)

            def hidden_proj(g, ms):
                for m in ms:
                    if m % HALF == 0:
                        wait(pe, taken["zproj"], halves(g, m // HALF))
                    by_rows("hproj", ps_odd, "w_h", parts(x_parts), m)

            def cond(g, ms):
                for m in ms:
                    if m == 0:
                        pe.wait_ge(xs_ready, halves(g - 1, 1))
                    if m % HALF == 0:
                        pe.wait_ge(taken["attn"], halves(g - 1, m // HALF))
                    by_rows("cond", ps_even, "cond", parts(a_parts), m)

            def key(g, ks, gru=True):
                for k in ks:
                    if k == 0:
                        if gru:
                            pe.wait_ge(taken["hproj"], halves(g, 1))
                        else:
                            pe.wait_ge(taken["value"], halves(g - 2, 1))
                    if k % HALF == 0:
                        pe.wait_ge(xk_ready, halves(g - 1, k // HALF))
                    by_cols("key", ps_odd, "key", parts(b_parts), k)

            def gate(g, ks):
                for k in ks:
                    if k == 0:
                        pe.wait_ge(taken["cond"], halves(g - 1, 1))
                    if k % HALF == 0:
                        pe.wait_ge(xr_ready, halves(g - 1, k // HALF))
                    by_cols("gate", ps_even, "gate", parts(x_parts), k)

            def value(g, ks):
                for k in ks:
                    if k == 0:
                        weights_split(pe, "value")
                        pe.wait_ge(taken["key"], halves(g - 1, 1))
                    if k % HALF == 0:
                        pe.wait_ge(kact_ready, halves(g - 1, k // HALF))
                    by_cols("value", ps_odd, "value", parts(a_parts), k)

            def reset_proj(g, ms, tail=True):
                for m in ms:
                    if m == 0:
                        pe.wait_ge(x_ready, halves(g + 1, 1))
                    if m % HALF == 0 and tail:
                        pe.wait_ge(taken["gate"], halves(g - 1, m // HALF))
                    if m % HALF == 0 and not tail:
                        wait(pe, taken["rproj"], halves(g, m // HALF))
                    by_rows("rproj", ps_even, "w_r", parts(x_parts), m)

            def update_proj(g, ms, tail=True):
                for m in ms:
                    if m % HALF == 0 and tail:
                        pe.wait_ge(taken["value"], halves(g - 1, m // HALF))
                    if m % HALF == 0 and not tail:
                        wait(pe, taken["hproj"], halves(g, m // HALF))
                    by_rows("zproj", ps_odd, "w_z", parts(x_parts), m)

            def window(g, gru=True, tail=True, proj=True):
                every = range(KT)
                if gru:
                    reset_update(g, 0)
                if tail:
                    attn(g, every, gru)
                if gru:
                    hidden_proj(g, every)
                    candidate(g, 0)
                if tail:
                    cond(g, every)
                if gru:
                    reset_update(g, 1)
                if tail:
                    key(g, range(0, 3), gru)
                if gru:
                    candidate(g, 1)
                if tail:
                    key(g, range(3, 4), gru)
                    gate(g, range(0, 2))
                if gru:
                    reset_update(g, 2)
                if tail:
                    gate(g, range(2, 4))
                    value(g, range(0, 1))
                if gru:
                    candidate(g, 2)
                if tail:
                    value(g, range(1, 4))
                if gru:
                    reset_update(g, 3)
                if proj:
                    reset_proj(g, every, tail)
                if gru:
                    candidate(g, 3)
                if proj:
                    update_proj(g, every, tail)

            def condition(name, ps):
                w = staged(pe, name)
                for m in range(KT):
                    for k in range(KT):
                        mm = pe.matmul(ps[:, m], w[:, k, m * P:(m + 1) * P], ys[:, k], start=k == 0, stop=k == KT - 1)
                mm.then_inc(cgate_acc, 1)

            pe.wait_ge(consts_done, 3)
            pe.wait_ge(bias_done, 1)
            for m in range(KT):
                mm = pe.matmul(ps_odd[1][:, 0, m:m + 1], bias_sum[:, m * P:(m + 1) * P], one[0:1, :],
                               start=True, stop=True)
            mm.then_inc(bias_acc, 1)
            pe.wait_ge(small_in, 48)
            pe.wait_ge(x_ready, halves(0, 1))
            weights_split(pe, "w_r")
            for m in range(KT):
                by_rows("rproj", ps_even, "w_r", parts(x_parts), m)
            condition("c_r", ps_r)
            weights_split(pe, "w_z")
            pe.wait_ge(bias_col, 1)
            for m in range(KT):
                by_rows("zproj", ps_odd, "w_z", parts(x_parts), m)
            condition("c_z", ps_z)
            condition("c_h", ps_c)
            pe.wait_ge(cgate_taken, len(WC))
            pe.wait_ge(cleared, 2)
            weights_split(pe, "u_h")
            reset_update(0, 0)
            hidden_proj(0, range(KT))
            candidate(0, 0)
            reset_update(0, 1)
            candidate(0, 1)
            reset_update(0, 2)
            candidate(0, 2)
            pe.wait_ge(taken["rproj"], halves(0, 0))
            pe.wait_ge(sq_done, 1)
            pe.wait_ge(ysq_done, 2)
            w = slots[SLOT_OF["cond_sq"]]
            for m in range(KT):
                for k in range(KT):
                    mm = pe.matmul(ps_even[0][:, 0, m * B:(m + 1) * B], w[:, k, m * P:(m + 1) * P], ysq[:, k],
                                   start=k == 0, stop=k == KT - 1)
            mm.then_inc(demod_acc, 1)
            reset_update(0, 3)
            pe.wait_ge(demod_done, 1)
            reset_proj(0, range(KT), tail=False)
            candidate(0, 3)
            update_proj(0, range(KT), tail=False)
            weights_split(pe, "gate")
            with pe.Fori(1, WINDOWS - 1) as g:
                window(g)
            window(WINDOWS - 1, proj=False)
            window(WINDOWS, gru=False, proj=False)

        @block.scalar
        def _(act):
            def sigmoid(buf, pre, done, n):
                act.wait_ge(pre, n)
                act.activation(buf, buf, ACT.Sigmoid).then_inc(done, 1)

            def gates(g, s):
                n = STEPS * g + s + 1
                sigmoid(rg, r_pre, r_sig, n)
                sigmoid(zg, z_pre, z_sig, n)

            def tanh(g, s):
                n = STEPS * g + s + 1
                act.wait_ge(c_pre, n)
                act.activation(hc, hc, ACT.Tanh).then_inc(c_tanh, 1)

            def take_attn(q, h):
                if h == 0:
                    wait(act, out_ready, halves(q - 1, 1))
                act.wait_ge(acc["attn"], halves(q, h))
                for m in range(HALF):
                    a = act.activation(y_now[:, HALF * h + m], ps_even[h][:, m], ACT.Identity,
                                       bias=attn_bias[:, HALF * h + m:HALF * h + m + 1],
                                       scale=unscale[:, W16.index("attn"):W16.index("attn") + 1])
                a.then_inc(taken["attn"], 1)

            def split_hi(dst, src, ready, done, q, h):
                act.wait_ge(ready, halves(q, h))
                act.copy(half(dst[:, 0], h), half(src, h)).then_inc(done, 1)

            def prev(q, h, mu, done, last_reader):
                wait(act, last_reader, halves(q, h))
                if last_reader is x_ready:
                    act.wait_ge(taken["cond"], halves(q, h))
                for m in range(HALF * h, HALF * h + HALF):
                    act.mul(raw[:, m], y_shift[:, m], rest[:, mu, m:m + 1]).then_inc(done, 1)

            def keep_last(q):
                act.wait_ge(prev_r_tile, KT * (q + 1))
                act.copy(yy[:, :, 0:B], yy[:, :, N:YW]).then_inc(y_kept, 1)

            def relu(q, h):
                act.wait_ge(acc["key"], halves(q, h))
                act.wait_ge(xr_ready, halves(q, h))
                act.activation(half(raw, h), ps_odd[h][:, :, :], ACT.Relu).then_inc(taken["key"], 1)

            def take_gate(q, h):
                act.wait_ge(y_kept, q + 1)
                act.wait_ge(acc["gate"], halves(q, h))
                act.activation(half(y_now, h), ps_even[h][:, :, :], ACT.Sigmoid).then_inc(taken["gate"], 1)

            def split_x(g, h, tail=True):
                act.wait_ge(raw_in[h], 16 * (g + 1))
                if tail:
                    act.wait_ge(acc["gate"], halves(g - 2, 1))
                elif g > 0:
                    act.wait_ge(acc["hproj"], halves(g - 1, 1))
                act.copy(half(x_parts[:, 0], h), half(raw, h)).then_inc(x_hi, 1)

            def window(g, gru=True, tail=True, proj=True):
                q = g - 1
                if gru:
                    gates(g, 0)
                if tail:
                    take_attn(q, 0)
                    take_attn(q, 1)
                    split_hi(a_parts, y_now, xs_done, xs_hi, q, 0)
                    split_hi(a_parts, y_now, xs_done, xs_hi, q, 1)
                if gru:
                    tanh(g, 0)
                if tail:
                    prev(q, 0, MU_K, prev_k_tile, x_ready)
                    split_hi(b_parts, raw, mix_k, xk_hi, q, 0)
                    prev(q, 1, MU_K, prev_k_tile, x_ready)
                if gru:
                    sigmoid(rg, r_pre, r_sig, STEPS * g + 2)
                if tail:
                    split_hi(b_parts, raw, mix_k, xk_hi, q, 1)
                    prev(q, 0, MU_R, prev_r_tile, xk_ready)
                if gru:
                    sigmoid(zg, z_pre, z_sig, STEPS * g + 2)
                if tail:
                    split_hi(x_parts, raw, mix_r, xr_hi, q, 0)
                    prev(q, 1, MU_R, prev_r_tile, xk_ready)
                if gru:
                    tanh(g, 1)
                if tail:
                    split_hi(x_parts, raw, mix_r, xr_hi, q, 1)
                    keep_last(q)
                    relu(q, 0)
                    relu(q, 1)
                    split_hi(a_parts, raw, relu_sq, kact_hi, q, 0)
                    split_hi(a_parts, raw, relu_sq, kact_hi, q, 1)
                if gru:
                    gates(g, 2)
                if tail:
                    take_gate(q, 0)
                    take_gate(q, 1)
                if gru:
                    tanh(g, 2)
                if proj:
                    split_x(g + 1, 0, tail)
                    split_x(g + 1, 1, tail)
                if gru:
                    gates(g, 3)
                    tanh(g, 3)

            def split_weight(name):
                w = staged(act, name)
                if name in W16:
                    i = W16.index(name)
                    act.wait_ge(scale_done, 2 * MAX_ORDER.index(name) + 1)
                    act.mul(wt[name][:, 0], w, wscale[:, i:i + 1]).then_inc(w_hi, 1)
                else:
                    act.copy(wt[name][:, 0], w).then_inc(w_hi, 1)

            def condition(name, ps, b):
                act.wait_ge(cgate_acc, WC.index(name) + 1)
                for m in range(KT):
                    a = act.activation(cond_v[name][:, m], ps[:, m], ACT.Identity, bias=vec[:, b, m:m + 1])
                a.then_inc(cgate_taken, 1)

            split_x(0, 0, tail=False)
            split_x(0, 1, tail=False)
            act.wait_ge(small_in, 48)
            act.wait_ge(bias_acc, 1)
            act.copy(attn_bias[:, :], ps_odd[1][:, 0, 0:KT]).then_inc(bias_col, 1)
            split_weight("w_r")
            split_weight("u_r")
            split_weight("w_z")
            condition("c_r", ps_r, B_R)
            split_weight("u_z")
            split_weight("w_h")
            condition("c_z", ps_z, B_Z)
            split_weight("u_h")
            condition("c_h", ps_c, B_H)
            gates(0, 0)
            tanh(0, 0)
            gates(0, 1)
            tanh(0, 1)
            gates(0, 2)
            split_weight("attn")
            tanh(0, 2)
            split_weight("cond")
            act.wait_ge(demod_done, 1)
            act.activation(droot, dvar, ACT.Sqrt).then_inc(root_done, 1)
            split_weight("key")
            split_x(1, 0, tail=False)
            split_x(1, 1, tail=False)
            gates(0, 3)
            split_weight("gate")
            tanh(0, 3)
            split_weight("value")
            with act.Fori(1, WINDOWS - 1) as g:
                window(g)
            window(WINDOWS - 1, proj=False)
            window(WINDOWS, gru=False, proj=False)

        @block.gpsimd
        def _(pool):
            for n, name in enumerate(MAX_ORDER):
                i = W16.index(name)
                pool.wait_ge(max_done, n + 1)
                pool.partition_all_reduce(wtop[:, i:i + 1], wmax[:, i:i + 1], P, RMAX).then_inc(top_done, 1)

            def square(q, h):
                pool.wait_ge(taken["key"], halves(q, h))
                pool.tensor_tensor(half(raw, h), half(raw, h), half(raw, h), ALU.mult).then_inc(relu_sq, 1)

            def residual(q, h):
                pool.wait_ge(taken["value"], halves(q, h))
                pool.tensor_tensor(half(x2, h), half(x2, h), half(y_now, h), ALU.add).then_inc(out_ready, 1)

            def window(g):
                for stage_of in (square, residual):
                    for h in range(2):
                        stage_of(g - 1, h)

            with pool.Fori(1, WINDOWS + 1) as g:
                window(g)

        @block.vector
        def _(dve):
            def add_projection(dst, ps, w, name, proj, g, s, acc_sem, done):
                if s == 0:
                    dve.wait_ge(taken[name], halves(g, 1))
                dve.wait_ge(acc_sem, STEPS * g + s + 1)
                i = W16.index(w)
                dve.scalar_tensor_tensor(dst, ps, unscale[:, i:i + 1], at_step(proj, s), ALU.mult, ALU.add).then_inc(done, 1)

            def reset_pre(g, s):
                add_projection(rg, ps_r, "u_r", "rproj", rproj, g, s, r_acc, r_pre)

            def reset_mul(g, s):
                dve.wait_ge(r_sig, STEPS * g + s + 1)
                dve.tensor_tensor(rg, rg, state, ALU.mult).then_inc(rh_full, 1)

            def reset_split(g, s):
                n = STEPS * g + s + 1
                dve.wait_ge(rh_full, n)
                dve.tensor_copy(rh_parts[:, 0], rg).then_inc(rh_hi, 1)
                dve.wait_ge(rh_hi, n)
                dve.tensor_tensor(rh_parts[:, 1], rg, rh_parts[:, 0], ALU.subtract).then_inc(rh_ready, 1)

            def reset(g, s):
                reset_pre(g, s)
                reset_mul(g, s)
                reset_split(g, s)

            def update(g, s):
                add_projection(zg, ps_z, "u_z", "zproj", zproj, g, s, z_acc, z_pre)

            def candidate_pre(g, s):
                add_projection(hc, ps_c, "u_h", "hproj", hproj, g, s, c_acc, c_pre)

            def blend(g, s):
                n = STEPS * g + s + 1
                dve.wait_ge(c_tanh, n)
                dve.scalar_tensor_tensor(hc, hc, STATE_SCALE, state, ALU.mult, ALU.subtract).then_inc(diff_done, 1)
                dve.wait_ge(diff_done, n)
                dve.wait_ge(z_sig, n)
                dve.tensor_tensor(hc, hc, zg, ALU.mult).then_inc(zdiff_done, 1)
                dve.wait_ge(zdiff_done, n)
                dve.tensor_tensor(state, state, hc, ALU.add).then_inc(state_done, 1)
                dve.wait_ge(state_done, n)
                dve.tensor_copy(hist[:, 0, :, s], state).then_inc(h_hi, 1)
                dve.wait_ge(h_hi, n)
                dve.tensor_tensor(hist[:, 1, :, s], state, hist[:, 0, :, s], ALU.subtract).then_inc(h_ready, 1)

            def new_state(g, s):
                candidate_pre(g, s)
                blend(g, s)

            def take_proj(name, g, h, dst, ps, v):
                dve.wait_ge(acc[name], halves(g, h))
                dve.tensor_tensor(by_time(half(dst, h)), by_time(ps[h]), over_time(half(cond_v[v], h)), ALU.add)\
                    .then_inc(taken[name], 1)

            def take_rproj(g, h):
                take_proj("rproj", g, h, rproj, ps_even, "c_r")

            def take_zproj(g, h):
                take_proj("zproj", g, h, zproj, ps_odd, "c_z")

            def take_hproj(g, h):
                take_proj("hproj", g, h, hproj, ps_odd, "c_h")

            def split_lo(dst, src, hi, done, q, h):
                dve.wait_ge(hi, halves(q, h))
                dve.tensor_tensor(half(dst[:, 1], h), half(src, h), half(dst[:, 0], h).bitcast(F32), ALU.subtract)\
                    .then_inc(done, 1)

            def style(q, h):
                dve.wait_ge(taken["attn"], halves(q, h))
                dve.wait_ge(res_in[h], 16 * (q + 1))
                dve.tensor_tensor(half(x2, h), half(x2, h), half(y_now, h), ALU.add).then_inc(x2_done, 1)
                dve.wait_ge(x2_done, halves(q, h))
                dve.tensor_tensor(by_time(half(y_now, h)), by_time(half(x2, h)), over_time(half(ys, h)), ALU.mult)\
                    .then_inc(xs_done, 1)

            def take_cond(q, h):
                dve.wait_ge(acc["cond"], halves(q, h))
                dve.tensor_tensor(by_time(half(y_now, h)), by_time(ps_even[h]), over_time(half(demod, h)), ALU.mult)\
                    .then_inc(taken["cond"], 1)

            def mix(q, h, mu, prev_tile, done):
                dve.wait_ge(taken["cond"], halves(q, h))
                for m in range(HALF * h, HALF * h + HALF):
                    dve.wait_ge(prev_tile, KT * q + m + 1)
                    d = dve.scalar_tensor_tensor(raw[:, m], y_now[:, m], vec[:, mu, m:m + 1], raw[:, m],
                                                 ALU.mult, ALU.add)
                d.then_inc(done, 1)

            def take_value(q, h):
                dve.wait_ge(acc["value"], halves(q, h))
                dve.wait_ge(taken["gate"], halves(q, h))
                dve.tensor_tensor(half(y_now, h), half(y_now, h), ps_odd[h][:, :, :], ALU.mult)\
                    .then_inc(taken["value"], 1)

            def window(g, gru=True, tail=True, proj=True):
                q = g - 1
                if gru:
                    reset(g, 0)
                    update(g, 0)
                if tail:
                    style(q, 0)
                    style(q, 1)
                    split_lo(a_parts, y_now, xs_hi, xs_ready, q, 0)
                    split_lo(a_parts, y_now, xs_hi, xs_ready, q, 1)
                if gru:
                    take_hproj(g, 0)
                    take_hproj(g, 1)
                    new_state(g, 0)
                if tail:
                    take_cond(q, 0)
                    mix(q, 0, MU_K, prev_k_tile, mix_k)
                    split_lo(b_parts, raw, xk_hi, xk_ready, q, 0)
                    take_cond(q, 1)
                if gru:
                    reset_pre(g, 1)
                if tail:
                    mix(q, 1, MU_K, prev_k_tile, mix_k)
                if gru:
                    reset_mul(g, 1)
                if tail:
                    split_lo(b_parts, raw, xk_hi, xk_ready, q, 1)
                if gru:
                    reset_split(g, 1)
                if tail:
                    mix(q, 0, MU_R, prev_r_tile, mix_r)
                if gru:
                    update(g, 1)
                if tail:
                    split_lo(x_parts, raw, xr_hi, xr_ready, q, 0)
                if gru:
                    candidate_pre(g, 1)
                if tail:
                    mix(q, 1, MU_R, prev_r_tile, mix_r)
                if gru:
                    blend(g, 1)
                if tail:
                    split_lo(x_parts, raw, xr_hi, xr_ready, q, 1)
                    for h in range(2):
                        split_lo(a_parts, raw, kact_hi, kact_ready, q, h)
                if gru:
                    reset(g, 2)
                    update(g, 2)
                    new_state(g, 2)
                if proj:
                    split_lo(x_parts, raw, x_hi, x_ready, g + 1, 0)
                    split_lo(x_parts, raw, x_hi, x_ready, g + 1, 1)
                if tail:
                    take_value(q, 0)
                    take_value(q, 1)
                if gru:
                    reset(g, 3)
                    update(g, 3)
                if proj:
                    take_rproj(g + 1, 0)
                    take_rproj(g + 1, 1)
                if gru:
                    new_state(g, 3)
                if proj:
                    take_zproj(g + 1, 0)
                    take_zproj(g + 1, 1)

            def largest(name):
                i = W16.index(name)
                dve.tensor_reduce(wmax[:, i:i + 1], staged(dve, name).rearrange("p k m -> p (k m)"), AX_X, ALU.max,
                                  apply_absolute_value=True).then_inc(max_done, 1)

            def scale(name):
                i, n = W16.index(name), MAX_ORDER.index(name)
                dve.wait_ge(top_done, n + 1)
                dve.tensor_scalar(wtop[:, i:i + 1], wtop[:, i:i + 1], TINY, None, ALU.max).then_inc(pow_done, 1)
                dve.wait_ge(pow_done, 3 * n + 1)
                dve.tensor_scalar(wpow[:, i:i + 1].bitcast(U32), wtop[:, i:i + 1].bitcast(U32), EXPONENT, None,
                                  ALU.bitwise_and).then_inc(pow_done, 1)
                dve.wait_ge(pow_done, 3 * n + 2)
                dve.reciprocal(wrec[:, i:i + 1], wpow[:, i:i + 1]).then_inc(pow_done, 1)
                dve.wait_ge(pow_done, 3 * n + 3)
                dve.tensor_scalar(wscale[:, i:i + 1], wrec[:, i:i + 1], WEIGHT_TOP, None, ALU.mult).then_inc(scale_done, 1)
                dve.tensor_scalar(unscale[:, i:i + 1], wpow[:, i:i + 1], 1.0 / (WEIGHT_TOP * STATE_SCALE), None,
                                  ALU.mult).then_inc(scale_done, 1)

            def split_weight(name):
                w, w_split = staged(dve, name), wt[name]
                dve.wait_ge(w_hi, SPLIT_ORDER.index(name) + 1)
                if name in W16:
                    i = W16.index(name)
                    dve.wait_ge(scale_done, 2 * MAX_ORDER.index(name) + 2)
                    dve.scalar_tensor_tensor(w_split[:, 1].rearrange("p k m -> p (k m)"),
                                             w.rearrange("p k m -> p (k m)"), wscale[:, i:i + 1],
                                             w_split[:, 0].rearrange("p k m -> p (k m)"), ALU.mult, ALU.subtract)\
                        .then_inc(w_lo, 1)
                else:
                    dve.tensor_tensor(w_split[:, 1], w, w_split[:, 0].bitcast(F32), ALU.subtract).then_inc(w_lo, 1)

            dve.memset(zero[:, :], 0.0).then_inc(consts_done, 1)
            dve.memset(one[:, :], 1.0).then_inc(consts_done, 1)
            dve.memset(hist[:, :, :, STEPS - 1], 0.0).then_inc(cleared, 1)
            dve.wait_ge(small_in, 48)
            dve.tensor_scalar(rest[:, :, :], vec[:, :, :], -1.0, 1.0, ALU.mult, ALU.add).then_inc(consts_done, 1)
            dve.wait_ge(consts_done, 1)
            dve.tensor_tensor_scan(bias_sum, zero[0:1, :].broadcast_to([1, D]), bias_in, 0.0, ALU.add, ALU.add)\
                .then_inc(bias_done, 1)
            split_lo(x_parts, raw, x_hi, x_ready, 0, 0)
            split_lo(x_parts, raw, x_hi, x_ready, 0, 1)
            split_weight("w_r")
            largest("u_r")
            scale("u_r")
            split_weight("u_r")
            split_weight("w_z")
            largest("u_z")
            scale("u_z")
            split_weight("u_z")
            split_weight("w_h")
            largest("u_h")
            scale("u_h")
            dve.wait_ge(cgate_acc, 3)
            dve.wait_ge(cgate_taken, 2)
            take_rproj(0, 0)
            take_rproj(0, 1)
            take_zproj(0, 0)
            take_zproj(0, 1)
            split_weight("u_h")
            dve.wait_ge(bias_acc, 1)
            dve.memset(state, 0.0).then_inc(cleared, 1)
            dve.wait_ge(cleared, 2)
            dve.wait_ge(cgate_taken, 3)
            reset(0, 0)
            update(0, 0)
            dve.tensor_scalar(ys[:, :, :], ys[:, :, :], YS_SCALE, None, ALU.mult).then_inc(ysq_done, 1)
            take_hproj(0, 0)
            take_hproj(0, 1)
            new_state(0, 0)
            dve.wait_ge(ysq_done, 1)
            dve.tensor_tensor(ysq, ys[:, :, :], ys[:, :, :], ALU.mult).then_inc(ysq_done, 1)
            w = staged(dve, "attn")
            for k in range(KT):
                d = dve.tensor_tensor_scan(w[:, k], zero[:, :].broadcast_to([P, D]), w[:, k], 0.0, ALU.add, ALU.add)
                if k == HALF - 1:
                    reset(0, 1)
                    update(0, 1)
            d.then_inc(scan_done, 1)
            dve.wait_ge(scan_done, 1)
            largest("attn")
            new_state(0, 1)
            scale("attn")
            w = staged(dve, "cond")
            dve.wait_ge(x_ready, halves(0, 1))
            dve.tensor_tensor(slots[SLOT_OF["cond_sq"]], w, w, ALU.mult).then_inc(sq_done, 1)
            reset(0, 2)
            update(0, 2)
            split_weight("attn")
            new_state(0, 2)
            split_weight("cond")
            dve.wait_ge(demod_acc, 1)
            dve.tensor_scalar(dvar, ps_even[0][:, 0].rearrange("p (k b) -> p k b", k=KT), EPS, None, ALU.add)\
                .then_inc(demod_done, 1)
            dve.wait_ge(root_done, 1)
            dve.reciprocal(dinv, droot).then_inc(demod_done, 1)
            dve.wait_ge(demod_done, 2)
            dve.tensor_tensor(dtmp, dinv, dinv, ALU.mult).then_inc(demod_done, 1)
            dve.wait_ge(demod_done, 3)
            dve.tensor_tensor(dtmp, dtmp, dvar, ALU.mult).then_inc(demod_done, 1)
            dve.wait_ge(demod_done, 4)
            dve.tensor_scalar(dtmp, dtmp, -0.5, 1.5, ALU.mult, ALU.add).then_inc(demod_done, 1)
            dve.wait_ge(demod_done, 5)
            dve.tensor_tensor(demod[:, :, :], dinv, dtmp, ALU.mult).then_inc(demod_done, 1)
            dve.wait_ge(demod_done, 6)
            reset(0, 3)
            update(0, 3)
            split_lo(x_parts, raw, x_hi, x_ready, 1, 0)
            split_lo(x_parts, raw, x_hi, x_ready, 1, 1)
            split_weight("key")
            take_rproj(1, 0)
            take_rproj(1, 1)
            new_state(0, 3)
            split_weight("gate")
            take_zproj(1, 0)
            take_zproj(1, 1)
            split_weight("value")
            dve.memset(yy[:, :, 0:B], 0.0).then_inc(cleared, 1)
            dve.wait_ge(cleared, 3)
            with dve.Fori(1, WINDOWS - 1) as g:
                window(g)
            window(WINDOWS - 1, proj=False)
            window(WINDOWS, gru=False, proj=False)


def kernel(**inputs):
    import concourse.bacc as bacc
    from concourse.bass_utils import run_bass_kernel_spmd as run

    f32 = {n: np.ascontiguousarray(a) for n, a in inputs.items()}

    def weight(name, turned=False):
        a = f32[name].T if turned else f32[name]
        return np.ascontiguousarray(a.reshape(KT, P, D).transpose(1, 0, 2))

    def columns(a):
        return a.reshape(KT, P, -1).transpose(1, 0, 2).reshape(P, -1)

    arrays = {
        "x": np.ascontiguousarray(f32["x"].reshape(B, WINDOWS, STEPS, KT, P).transpose(1, 4, 3, 2, 0).reshape(WINDOWS, P, KT, N)),
        "small": np.ascontiguousarray(np.concatenate(
            [columns(f32[n]) for n in ("L0_cond_b_r", "L0_cond_b_z", "L0_cond_b", "L0_ffn_mu_r", "L0_ffn_mu_k")]
            + [columns(f32["cond_1024"].T)], axis=1)),
        "bias_row": f32["L0_attn_bias"].reshape(1, D),
    }
    sources = {
        "c_r": ("L0_cond_C_r",), "c_z": ("L0_cond_C_z",), "c_h": ("L0_cond_C",),
        "u_r": ("L0_cond_U_r",), "u_z": ("L0_cond_U_z",), "u_h": ("L0_cond_U",),
        "w_r": ("L0_cond_W_r",), "w_z": ("L0_cond_W_z",), "w_h": ("L0_cond_W",),
        "cond": ("L0_cond2_weight",), "attn": ("L0_attn_W", True),
        "key": ("L0_ffn_W_k", True), "gate": ("L0_ffn_W_r", True), "value": ("L0_ffn_W_v", True),
    }
    for name, source in sources.items():
        arrays["raw_" + name] = weight(*source)

    nc = bacc.Bacc("TRN2", target_bir_lowering=False, num_devices=1)
    sources = {n: sources[n] for n in SLOT_OF if n in sources}
    dram = {n: nc.dram_tensor(n, a.shape, F32, kind="ExternalInput").ap() for n, a in arrays.items()}
    out = nc.dram_tensor("out", (WINDOWS, P, KT, N), F32, kind="ExternalOutput").ap()
    gru_ffn_kernel(nc, dram["x"], {n: dram["raw_" + n] for n in sources}, dram["small"], dram["bias_row"], out)
    r = run(nc, [arrays], core_ids=[0])
    y = np.asarray(r.results[0]["out"]).reshape(WINDOWS, P, KT, STEPS, B)
    return np.ascontiguousarray(y.transpose(4, 0, 3, 2, 1)).reshape(B, T, D)
```

```python
from contextlib import ExitStack

import numpy as np

import concourse.bass as bass
from concourse import mybir

F32 = mybir.dt.float32
F32R = mybir.dt.float32r
F16 = mybir.dt.float16
U32 = mybir.dt.uint32
ALU = mybir.AluOpType
ACT = mybir.ActivationFunctionType
AX_X = mybir.AxisListType.X
RMAX = bass.bass_isa.ReduceOp.max

P = 128
B, T, D = 64, 128, 512
KT = D // P
STEPS = 4
WINDOWS = T // STEPS
N = STEPS * B
HALF = KT // 2
STATE_SCALE = 2.0 ** 14
WEIGHT_TOP = 2.0 ** 14
TINY = 2.0 ** -90
EXPONENT = 0x7F800000
PASSES = ((0, 0), (0, 1), (1, 0))
EPS = 1e-08
YS_SCALE = float(np.float32(1.0) / np.sqrt(np.float32(D)))

W16 = ["attn", "u_r", "u_z", "u_h"]
W32 = ["cond", "key", "gate", "value", "w_r", "w_z", "w_h"]
WC = ["c_z", "c_r", "c_h"]
SLOT_OF = {"c_z": 0, "w_z": 2, "c_h": 1, "w_h": 3, "c_r": 2, "u_r": 4, "w_r": 3, "u_z": 2, "u_h": 4,
           "attn": 3, "cond": 2, "cond_sq": 2, "gate": 4, "value": 4, "key": 2}
SPLIT_ORDER = ["w_z", "w_h", "u_r", "w_r", "u_z", "u_h", "cond", "gate", "attn", "value", "key"]
LOW_BY = {"dve": ["w_z", "u_r", "u_z", "u_h", "attn"],
          "pool": ["w_h", "w_r", "cond", "gate", "value", "key"]}
MAX_ORDER = [n for n in SPLIT_ORDER if n in W16]
B_R, B_Z, B_H, MU_R, MU_K = range(5)
NVEC = 5
PRODUCTS = ["attn", "hproj", "cond", "key", "gate", "value", "rproj", "zproj"]


def gru_ffn_kernel(nc, x, weights, small, bias_row, out):
    ctx = ExitStack()
    with ctx:
        def sb(name, shape, dt=F32):
            return ctx.enter_context(nc.sbuf_tensor(name, shape, dt))

        def sem(name):
            return ctx.enter_context(nc.semaphore(name))

        def psum(name, shape):
            return ctx.enter_context(nc.psum_tensor(name, shape, F32))

        wt = {n: sb("w_" + n, [P, 2, KT, D], F32R) for n in W32}
        wt |= {n: sb("w_" + n, [P, 2, KT, D], F16) for n in W16}
        x_parts = sb("x_parts", [P, 2, KT, N], F32R)
        with nc.sbuf_tensor("stage_ab", [P, 2, KT, D], F32) as stage_ab:
            pass
        a_parts = sb("a_parts", [P, 2, KT, N], F32R)
        b_parts = sb("b_parts", [P, 2, KT, N], F32R)
        hist = sb("hist", [P, 2, KT, STEPS, B], F16)
        rh_parts = sb("rh_parts", [P, 2, KT, B], F16)
        YW = (STEPS + 1) * B
        scratch = sb("scratch", [P, 5 * KT * N + KT * YW])
        bufs = scratch[:, 0:5 * KT * N].rearrange("p (i k n) -> p i k n", i=5, k=KT)
        rproj, zproj, x2, raw, hproj = (bufs[:, i] for i in range(5))
        yy = scratch[:, 5 * KT * N:5 * KT * N + KT * YW].rearrange("p (k n) -> p k n", k=KT)
        y_now = yy[:, :, B:YW]
        y_shift = yy[:, :, 0:N]
        def rows(first):
            return scratch[:, first * KT * N:first * KT * N + KT * D].rearrange("p (k m) -> p k m", k=KT)
        slots = [rows(0), rows(4), stage_ab[:, 0], stage_ab[:, 1], rows(2)]
        x_next = scratch[:, 5 * KT * N:6 * KT * N].rearrange("p (k n) -> p k n", k=KT)
        ysq = scratch[:, 6 * KT * N:6 * KT * N + KT * B].rearrange("p (k b) -> p k b", k=KT)
        dinv, dtmp = (stage_ab[:, 1, i, 0:KT * B].rearrange("p (k b) -> p k b", k=KT) for i in range(2))
        work = sb("work", [P, 4 * KT * B])
        rg, zg, hc, state = (work[:, i * KT * B:(i + 1) * KT * B].rearrange("p (k b) -> p k b", k=KT)
                             for i in range(4))
        kept = rg
        bias_in, bias_sum = work[0:1, 0:D], work[0:1, D:2 * D]
        cond_v = {n: sb("v_" + n, [P, KT, B]) for n in WC}
        ys = sb("ys", [P, KT, B])
        demod = sb("demod", [P, KT, B])
        vec = sb("vec", [P, NVEC, KT])
        rest = sb("rest", [P, NVEC, KT])
        attn_bias = sb("attn_bias", [P, KT])
        wmax = sb("wmax", [P, len(W16)])
        wtop = sb("wtop", [P, len(W16)])
        wpow = sb("wpow", [P, len(W16)])
        wrec = sb("wrec", [P, len(W16)])
        wscale = sb("wscale", [P, len(W16)])
        unscale = sb("unscale", [P, len(W16)])
        zero = sb("zero", [P, 1])
        one = sb("one", [P, 1])
        eps = sb("eps", [P, 1])

        ps_r, ps_z, ps_c = (psum("ps_" + n, [P, 2, KT, B]) for n in "rzc")
        ps_even = [psum(f"ps_even{h}", [P, HALF, N]) for h in range(2)]
        ps_demod = psum("ps_demod", [P, KT, B])
        ps_odd = [psum(f"ps_odd{h}", [P, HALF, N]) for h in range(2)]

        small_in = sem("small_in")
        stage_in = [sem(f"stage_in{i}") for i in range(len(slots))]
        consts_done, bias_done, bias_acc, bias_col = sem("consts_done"), sem("bias_done"), sem("bias_acc"), sem("bias_col")
        cgate_acc, cgate_taken = sem("cgate_acc"), sem("cgate_taken")
        scan_done, sq_done, demod_acc, demod_done = sem("scan_done"), sem("sq_done"), sem("demod_acc"), sem("demod_done")
        ysq_done, root_done = sem("ysq_done"), sem("root_done")
        max_done, top_done, pow_done, scale_done = sem("max_done"), sem("top_done"), sem("pow_done"), sem("scale_done")
        w_hi, w_lo = sem("w_hi"), {e: sem("w_lo_" + e) for e in LOW_BY}
        cleared = sem("cleared")
        r_acc, z_acc, c_acc = sem("r_acc"), sem("z_acc"), sem("c_acc")
        acc = {n: sem(n + "_acc") for n in PRODUCTS}
        taken = {n: sem(n + "_taken") for n in PRODUCTS}
        r_part, z_part, c_part = sem("r_part"), sem("z_part"), sem("c_part")
        r_pre, z_pre, c_pre = sem("r_pre"), sem("z_pre"), sem("c_pre")
        r_sig, z_sig, c_tanh = sem("r_sig"), sem("z_sig"), sem("c_tanh")
        rh_full, rh_hi, rh_ready = sem("rh_full"), sem("rh_hi"), sem("rh_ready")
        zh_done, kept_done, zc_done, state_done = sem("zh_done"), sem("kept_done"), sem("zc_done"), sem("state_done")
        h_hi, h_ready = sem("h_hi"), sem("h_ready")
        x_hi, x_ready = sem("x_hi"), sem("x_ready")
        x2_done, xs_done, xs_hi, xs_ready = sem("x2_done"), sem("xs_done"), sem("xs_hi"), sem("xs_ready")
        prev_k_tile, mix_k, xk_hi, xk_ready = sem("prev_k_tile"), sem("mix_k"), sem("xk_hi"), sem("xk_ready")
        prev_r_tile, mix_r, xr_hi, xr_ready = sem("prev_r_tile"), sem("mix_r"), sem("xr_hi"), sem("xr_ready")
        y_kept = sem("y_kept")
        relu_sq, kact_hi, kact_ready = sem("relu_sq"), sem("kact_hi"), sem("kact_ready")
        out_ready = sem("out_ready")
        raw_in = [sem(f"raw_in{h}") for h in range(2)]
        res_in = [sem(f"res_in{h}") for h in range(2)]
        out_stored = [sem(f"out_stored{h}") for h in range(2)]

        def wait(eng, semaphore, value):
            if not isinstance(value, int) or value > 0:
                eng.wait_ge(semaphore, value)

        def halves(g, h):
            return 2 * g + h + 1

        def steps(g, s):
            return STEPS * g + s + 1

        def products(g, s):
            return STEPS * g + s

        def half(buf, h):
            return buf[:, HALF * h:HALF * h + HALF]

        def over_time(a):
            k = a.shape[1]
            return a.unsqueeze(2).broadcast_to([P, k, STEPS, B])

        def by_time(a):
            return a.rearrange("p k (t b) -> p k t b", t=STEPS)

        def at_step(a, s):
            return a[:, :, s * B:(s + 1) * B]

        def occupants(name):
            names = list(SLOT_OF)
            return [n for n in names[:names.index(name)] if SLOT_OF[n] == SLOT_OF[name]]

        def staged(eng, name):
            loads = [n for n in occupants(name) if n in weights] + [name]
            eng.wait_ge(stage_in[SLOT_OF[name]], 16 * len(loads))
            return slots[SLOT_OF[name]]

        def used_up(eng, name):
            if name in WC:
                eng.wait_ge(cgate_acc, WC.index(name) + 1)
            elif name == "cond_sq":
                eng.wait_ge(demod_acc, 1)
            else:
                low_done(eng, name)

        def low_done(eng, name):
            for e, names in LOW_BY.items():
                if name in names:
                    eng.wait_ge(w_lo[e], names.index(name) + 1)

        def weights_split(eng, name):
            eng.wait_ge(w_hi, SPLIT_ORDER.index(name) + 1)
            low_done(eng, name)

        block = ctx.enter_context(nc.Block())

        @block.sync
        def _(sp):
            def load_raw(g, dst=raw):
                for h in range(2):
                    sp.dma_start(half(dst, h), x[g][:, HALF * h:HALF * h + HALF]).then_inc(raw_in[h], 16)

            def load_res(g):
                for h in range(2):
                    wait(sp, out_stored[h], 16 * g)
                    sp.dma_start(half(x2, h), x[g][:, HALF * h:HALF * h + HALF]).then_inc(res_in[h], 16)

            sp.dma_start(vec[:, :, :], small[:, 0:NVEC * KT]).then_inc(small_in, 16)
            sp.dma_start(ys[:, :, :], small[:, NVEC * KT:NVEC * KT + KT * B]).then_inc(small_in, 16)
            sp.dma_start(bias_in, bias_row).then_inc(small_in, 16)
            load_raw(0)
            for name in weights:
                if name == "u_r":
                    sp.wait_ge(x_ready, halves(0, 1))
                if name == "attn":
                    used_up(sp, "c_h")
                    load_raw(1, x_next)
                if occupants(name):
                    used_up(sp, occupants(name)[-1])
                sp.dma_start(slots[SLOT_OF[name]], weights[name]).then_inc(stage_in[SLOT_OF[name]], 16)
            used_up(sp, "value")
            load_res(0)

            def window(g, gru=True, proj=True):
                if proj:
                    sp.wait_ge(kact_ready, halves(g - 1, 1))
                    load_raw(g + 1)
                for h in range(2):
                    sp.wait_ge(out_ready, halves(g - 1, h))
                    sp.dma_start(out[g - 1][:, HALF * h:HALF * h + HALF], half(x2, h)).then_inc(out_stored[h], 16)
                if gru:
                    load_res(g)

            with sp.Fori(1, WINDOWS - 1) as g:
                window(g)
            window(WINDOWS - 1, proj=False)
            window(WINDOWS, gru=False, proj=False)
            for h in range(2):
                sp.wait_ge(out_stored[h], 16 * WINDOWS)

        @block.tensor
        def _(pe):
            def tile_product(ps_tile, w, data, m, ks, first, last, **group):
                for k in ks:
                    for i, (wp, dp) in enumerate(PASSES):
                        mm = pe.matmul(ps_tile, w[:, wp, k, m * P:(m + 1) * P], data(dp, k),
                                       start=first and k == ks[0] and i == 0,
                                       stop=last and k == ks[-1] and i == len(PASSES) - 1, **group)
                return mm

            def step_product(ps, w, data, done):
                for m in range(KT):
                    rows = slice(m * P, (m + 1) * P)
                    for k in range(KT):
                        pe.matmul(ps[:, :, m], wt[w][:, 0, k, rows], data(slice(0, 2), k), start=k == 0, stop=False)
                        mm = pe.matmul(ps[:, 0, m], wt[w][:, 1, k, rows], data(0, k), start=False, stop=k == KT - 1)
                mm.then_inc(done, 1)

            def reset_product(s):
                step_product(ps_r, "u_r", lambda dp, k: hist[:, dp, k, (s - 1) % STEPS], r_acc)

            def update_product(s):
                step_product(ps_z, "u_z", lambda dp, k: hist[:, dp, k, (s - 1) % STEPS], z_acc)

            def reset_update(g, s):
                pe.wait_ge(h_ready, steps(g, s) - 1)
                reset_product(s)
                update_product(s)

            def candidate(g, s):
                pe.wait_ge(rh_ready, products(g, s))
                step_product(ps_c, "u_h", lambda dp, k: rh_parts[:, dp, k], c_acc)

            def by_rows(name, ps, w, data, m):
                mm = tile_product(ps[m // HALF][:, m % HALF], wt[w], data, m, range(KT), True, True)
                if m % HALF == HALF - 1:
                    mm.then_inc(acc[name], 1)

            def by_cols(name, ps, w, data, k):
                for m in range(KT):
                    mm = tile_product(ps[m // HALF][:, m % HALF], wt[w], data, m, [k],
                                      k == 0 and m % HALF == 0, k == KT - 1, skip_group_check=True)
                    if k == KT - 1 and m % HALF == HALF - 1:
                        mm.then_inc(acc[name], 1)

            def parts(buf):
                return lambda dp, k: buf[:, dp, k]

            def attn(g, ms, gru=True):
                for m in ms:
                    if m % HALF == 0:
                        if gru:
                            pe.wait_ge(taken["rproj"], halves(g, m // HALF))
                        else:
                            pe.wait_ge(taken["gate"], halves(g - 2, m // HALF))
                            wait(pe, h_ready, STEPS * g)
                    by_rows("attn", ps_even, "attn", lambda dp, k: hist[:, dp, k].rearrange("p t b -> p (t b)"), m)

            def hidden_proj(g, ms):
                for m in ms:
                    if m % HALF == 0:
                        wait(pe, taken["zproj"], halves(g, m // HALF))
                    by_rows("hproj", ps_odd, "w_h", parts(x_parts), m)

            def cond(g, ms):
                for m in ms:
                    if m == 0:
                        pe.wait_ge(xs_ready, halves(g - 1, 1))
                    if m % HALF == 0:
                        pe.wait_ge(taken["attn"], halves(g - 1, m // HALF))
                    by_rows("cond", ps_even, "cond", parts(a_parts), m)

            def cond_by_cols(g):
                for k in range(KT):
                    if k == 0:
                        pe.wait_ge(taken["attn"], halves(g - 1, 1))
                    if k % HALF == 0:
                        pe.wait_ge(xs_ready, halves(g - 1, k // HALF))
                    by_cols("cond", ps_even, "cond", parts(a_parts), k)

            def key(g, ks, gru=True):
                for k in ks:
                    if k == 0:
                        if gru:
                            pe.wait_ge(taken["hproj"], halves(g, 1))
                        else:
                            pe.wait_ge(taken["value"], halves(g - 2, 1))
                    if k % HALF == 0:
                        pe.wait_ge(xk_ready, halves(g - 1, k // HALF))
                    by_cols("key", ps_odd, "key", parts(b_parts), k)

            def gate(g, ks):
                for k in ks:
                    if k == 0:
                        pe.wait_ge(taken["cond"], halves(g - 1, 1))
                    if k % HALF == 0:
                        pe.wait_ge(xr_ready, halves(g - 1, k // HALF))
                    by_cols("gate", ps_even, "gate", parts(x_parts), k)

            def value(g, ks):
                for k in ks:
                    if k == 0:
                        pe.wait_ge(taken["key"], halves(g - 1, 1))
                    if k % HALF == 0:
                        pe.wait_ge(kact_ready, halves(g - 1, k // HALF))
                    by_cols("value", ps_odd, "value", parts(a_parts), k)

            def reset_proj(g, ms, setup=False):
                for m in ms:
                    if m == 0:
                        pe.wait_ge(x_ready, halves(g + 1, 1))
                    if m % HALF == 0 and not setup:
                        pe.wait_ge(taken["gate"], halves(g - 1, m // HALF))
                    if m % HALF == 0 and setup:
                        wait(pe, taken["rproj"], halves(g, m // HALF))
                    by_rows("rproj", ps_even, "w_r", parts(x_parts), m)

            def update_proj(g, ms, setup=False):
                for m in ms:
                    if m % HALF == 0 and not setup:
                        pe.wait_ge(taken["value"], halves(g - 1, m // HALF))
                    if m % HALF == 0 and setup:
                        wait(pe, taken["hproj"], halves(g, m // HALF))
                    by_rows("zproj", ps_odd, "w_z", parts(x_parts), m)

            def window(g, gru=True, proj=True, first=False):
                every = range(KT)

                def ready(name):
                    if first:
                        weights_split(pe, name)

                if gru:
                    reset_update(g, 0)
                ready("attn")
                attn(g, every, gru)
                if gru:
                    hidden_proj(g, every)
                    candidate(g, 0)
                ready("cond")
                if gru:
                    cond(g, every)
                else:
                    cond_by_cols(g)
                if gru:
                    reset_update(g, 1)
                ready("key")
                key(g, range(0, 3), gru)
                if gru:
                    candidate(g, 1)
                key(g, range(3, 4), gru)
                ready("gate")
                gate(g, range(0, 2))
                if gru:
                    reset_update(g, 2)
                gate(g, range(2, 4))
                ready("value")
                value(g, range(0, 1))
                if gru:
                    candidate(g, 2)
                value(g, range(1, 4))
                if gru:
                    reset_update(g, 3)
                if proj:
                    reset_proj(g, every)
                if gru:
                    candidate(g, 3)
                if proj:
                    update_proj(g, every)

            def condition(name, ps):
                w = staged(pe, name)
                for m in range(KT):
                    for k in range(KT):
                        mm = pe.matmul(ps[:, 0, m], w[:, k, m * P:(m + 1) * P], ys[:, k], start=k == 0, stop=k == KT - 1)
                mm.then_inc(cgate_acc, 1)

            pe.wait_ge(consts_done, 4)
            pe.wait_ge(bias_done, 1)
            for m in range(KT):
                mm = pe.matmul(ps_odd[1][:, 0, m:m + 1], bias_sum[:, m * P:(m + 1) * P], one[0:1, :],
                               start=True, stop=True)
            mm.then_inc(bias_acc, 1)
            pe.wait_ge(small_in, 48)
            condition("c_z", ps_z)
            pe.wait_ge(x_ready, halves(0, 1))
            weights_split(pe, "w_z")
            pe.wait_ge(bias_col, 1)
            for m in range(KT):
                by_rows("zproj", ps_odd, "w_z", parts(x_parts), m)
            condition("c_r", ps_r)
            condition("c_h", ps_c)
            weights_split(pe, "w_h")
            hidden_proj(0, range(KT))
            weights_split(pe, "w_r")
            for m in range(KT):
                by_rows("rproj", ps_even, "w_r", parts(x_parts), m)
            pe.wait_ge(cgate_taken, len(WC))
            weights_split(pe, "u_r")
            pe.wait_ge(h_ready, 1)
            reset_product(1)
            weights_split(pe, "u_z")
            update_product(1)
            reset_proj(0, range(KT), setup=True)
            weights_split(pe, "u_h")
            candidate(0, 1)
            update_proj(0, range(0, 2), setup=True)
            reset_update(0, 2)
            update_proj(0, [2], setup=True)
            candidate(0, 2)
            pe.wait_ge(sq_done, 1)
            pe.wait_ge(ysq_done, 2)
            w = slots[SLOT_OF["cond_sq"]]
            for m in range(KT):
                for k in range(KT):
                    mm = pe.matmul(ps_demod[:, m], w[:, k, m * P:(m + 1) * P], ysq[:, k],
                                   start=k == 0, stop=k == KT - 1)
            mm.then_inc(demod_acc, 1)
            reset_update(0, 3)
            candidate(0, 3)
            update_proj(0, [3], setup=True)
            window(1, first=True)
            with pe.Fori(2, WINDOWS - 1) as g:
                window(g)
            window(WINDOWS - 1, proj=False)
            window(WINDOWS, gru=False, proj=False)

        @block.scalar
        def _(act):
            def sigmoid(buf, pre, done, n):
                act.wait_ge(pre, n)
                act.activation(buf, buf, ACT.Sigmoid).then_inc(done, 1)

            def reset_gate(g, s):
                sigmoid(rg, r_pre, r_sig, products(g, s))

            def update_gate(g, s):
                sigmoid(zg, z_pre, z_sig, products(g, s))

            def tanh(g, s):
                act.wait_ge(c_pre, products(g, s))
                act.activation(hc, hc, ACT.Tanh).then_inc(c_tanh, 1)

            def take_attn(q, h):
                if h == 0:
                    wait(act, out_ready, halves(q - 1, 1))
                act.wait_ge(acc["attn"], halves(q, h))
                for m in range(HALF):
                    a = act.activation(y_now[:, HALF * h + m], ps_even[h][:, m], ACT.Identity,
                                       bias=attn_bias[:, HALF * h + m:HALF * h + m + 1],
                                       scale=unscale[:, W16.index("attn"):W16.index("attn") + 1])
                a.then_inc(taken["attn"], 1)

            def split_hi(dst, src, ready, done, q, h):
                act.wait_ge(ready, halves(q, h))
                act.copy(half(dst[:, 0], h), half(src, h)).then_inc(done, 1)

            def prev(q, h, mu, done, last_reader):
                wait(act, last_reader, halves(q, h))
                if last_reader is x_ready:
                    act.wait_ge(taken["cond"], halves(q, h))
                for m in range(HALF * h, HALF * h + HALF):
                    act.mul(raw[:, m], y_shift[:, m], rest[:, mu, m:m + 1]).then_inc(done, 1)

            def keep_last(q):
                act.wait_ge(prev_r_tile, KT * (q + 1))
                act.copy(yy[:, :, 0:B], yy[:, :, N:YW]).then_inc(y_kept, 1)

            def relu(q, h):
                act.wait_ge(acc["key"], halves(q, h))
                act.wait_ge(xr_ready, halves(q, h))
                act.activation(half(raw, h), ps_odd[h][:, :, :], ACT.Relu).then_inc(taken["key"], 1)

            def take_gate(q, h):
                act.wait_ge(y_kept, q + 1)
                act.wait_ge(acc["gate"], halves(q, h))
                act.activation(half(y_now, h), ps_even[h][:, :, :], ACT.Sigmoid).then_inc(taken["gate"], 1)

            def split_x(g, h, setup=False, src=raw):
                act.wait_ge(raw_in[h], 16 * (g + 1))
                if not setup:
                    act.wait_ge(acc["gate"], halves(g - 2, 1))
                elif g > 0:
                    act.wait_ge(acc["rproj"], halves(g - 1, 1))
                act.copy(half(x_parts[:, 0], h), half(src, h)).then_inc(x_hi, 1)

            def window(g, gru=True, proj=True, first=False):
                q = g - 1
                if gru:
                    reset_gate(g, 0)
                    update_gate(g, 0)
                take_attn(q, 0)
                if not gru:
                    split_hi(a_parts, y_now, xs_done, xs_hi, q, 0)
                take_attn(q, 1)
                if first:
                    used_up(act, "key")
                if gru:
                    split_hi(a_parts, y_now, xs_done, xs_hi, q, 0)
                split_hi(a_parts, y_now, xs_done, xs_hi, q, 1)
                if gru:
                    tanh(g, 0)
                prev(q, 0, MU_K, prev_k_tile, x_ready)
                if first:
                    act.wait_ge(demod_done, 5)
                split_hi(b_parts, raw, mix_k, xk_hi, q, 0)
                prev(q, 1, MU_K, prev_k_tile, x_ready)
                if gru:
                    reset_gate(g, 1)
                split_hi(b_parts, raw, mix_k, xk_hi, q, 1)
                prev(q, 0, MU_R, prev_r_tile, xk_ready)
                if gru:
                    update_gate(g, 1)
                split_hi(x_parts, raw, mix_r, xr_hi, q, 0)
                prev(q, 1, MU_R, prev_r_tile, xk_ready)
                if gru:
                    tanh(g, 1)
                split_hi(x_parts, raw, mix_r, xr_hi, q, 1)
                keep_last(q)
                relu(q, 0)
                relu(q, 1)
                split_hi(a_parts, raw, relu_sq, kact_hi, q, 0)
                split_hi(a_parts, raw, relu_sq, kact_hi, q, 1)
                if gru:
                    reset_gate(g, 2)
                    update_gate(g, 2)
                take_gate(q, 0)
                take_gate(q, 1)
                if gru:
                    tanh(g, 2)
                if proj:
                    split_x(g + 1, 0)
                    split_x(g + 1, 1)
                if gru:
                    reset_gate(g, 3)
                    update_gate(g, 3)
                    tanh(g, 3)

            def split_weight(name):
                w = staged(act, name)
                if name in W16:
                    i = W16.index(name)
                    act.wait_ge(scale_done, 2 * MAX_ORDER.index(name) + 1)
                    act.mul(wt[name][:, 0], w, wscale[:, i:i + 1]).then_inc(w_hi, 1)
                else:
                    act.copy(wt[name][:, 0], w).then_inc(w_hi, 1)

            def condition(name, ps, b):
                act.wait_ge(cgate_acc, WC.index(name) + 1)
                for m in range(KT):
                    a = act.activation(cond_v[name][:, m], ps[:, 0, m], ACT.Identity, bias=vec[:, b, m:m + 1])
                a.then_inc(cgate_taken, 1)

            split_x(0, 0, setup=True)
            split_x(0, 1, setup=True)
            act.wait_ge(small_in, 48)
            act.wait_ge(bias_acc, 1)
            act.copy(attn_bias[:, :], ps_odd[1][:, 0, 0:KT]).then_inc(bias_col, 1)
            split_weight("w_z")
            condition("c_z", ps_z, B_Z)
            split_weight("w_h")
            condition("c_r", ps_r, B_R)
            split_weight("u_r")
            split_weight("w_r")
            condition("c_h", ps_c, B_H)
            act.wait_ge(taken["zproj"], halves(0, 1))
            act.activation(zg, at_step(zproj, 0), ACT.Sigmoid).then_inc(z_sig, 1)
            act.wait_ge(taken["hproj"], halves(0, 1))
            act.activation(hc, at_step(hproj, 0), ACT.Tanh).then_inc(c_tanh, 1)
            split_weight("u_z")
            split_x(1, 0, setup=True, src=x_next)
            split_x(1, 1, setup=True, src=x_next)
            split_weight("u_h")
            reset_gate(0, 1)
            update_gate(0, 1)
            split_weight("cond")
            tanh(0, 1)
            low_done(act, "cond")
            act.activation(slots[SLOT_OF["cond_sq"]], slots[SLOT_OF["cond"]], ACT.Square).then_inc(sq_done, 1)
            reset_gate(0, 2)
            update_gate(0, 2)
            split_weight("gate")
            tanh(0, 2)
            act.wait_ge(demod_acc, 1)
            act.activation(demod[:, :, :], ps_demod[:, :, :], ACT.Sqrt, bias=eps[:, :]).then_inc(root_done, 1)
            reset_gate(0, 3)
            update_gate(0, 3)
            split_weight("attn")
            tanh(0, 3)
            split_weight("value")
            split_weight("key")
            window(1, first=True)
            with act.Fori(2, WINDOWS - 1) as g:
                window(g)
            window(WINDOWS - 1, proj=False)
            window(WINDOWS, gru=False, proj=False)

        @block.gpsimd
        def _(pool):
            def largest(name):
                n, i = MAX_ORDER.index(name), W16.index(name)
                pool.wait_ge(max_done, n + 1)
                pool.partition_all_reduce(wtop[:, i:i + 1], wmax[:, i:i + 1], P, RMAX).then_inc(top_done, 1)

            def split_weight(name):
                w = staged(pool, name)
                pool.wait_ge(w_hi, SPLIT_ORDER.index(name) + 1)
                pool.tensor_tensor(wt[name][:, 1], w, wt[name][:, 0].bitcast(F32), ALU.subtract)\
                    .then_inc(w_lo["pool"], 1)

            def square(q, h):
                pool.wait_ge(taken["key"], halves(q, h))
                pool.tensor_tensor(half(raw, h), half(raw, h), half(raw, h), ALU.mult).then_inc(relu_sq, 1)

            def residual(q, h):
                pool.wait_ge(taken["value"], halves(q, h))
                pool.tensor_tensor(half(x2, h), half(x2, h), half(y_now, h), ALU.add).then_inc(out_ready, 1)

            def split_lo(dst, hi, done, q, h, src=raw):
                pool.wait_ge(hi, halves(q, h))
                pool.tensor_tensor(half(dst[:, 1], h), half(src, h), half(dst[:, 0], h).bitcast(F32), ALU.subtract)\
                    .then_inc(done, 1)

            def keep(g, s):
                n = products(g, s)
                pool.wait_ge(z_sig, steps(g, s))
                pool.wait_ge(rh_ready, n)
                pool.tensor_tensor(kept, zg, state, ALU.mult).then_inc(zh_done, 1)
                pool.wait_ge(zh_done, n)
                pool.tensor_tensor(kept, state, kept, ALU.subtract).then_inc(kept_done, 1)

            def window(g, gru=True):
                q = g - 1
                if gru:
                    keep(g, 0)
                    keep(g, 1)
                split_lo(x_parts, xr_hi, xr_ready, q, 1)
                for h in range(2):
                    square(q, h)
                for h in range(2):
                    split_lo(a_parts, kact_hi, kact_ready, q, h)
                if gru:
                    keep(g, 2)
                if gru:
                    for h in range(2):
                        residual(q, h)
                    keep(g, 3)

            split_weight("w_h")
            largest("u_r")
            split_weight("w_r")
            largest("u_z")
            largest("u_h")
            split_lo(x_parts, x_hi, x_ready, 1, 0, x_next)
            split_lo(x_parts, x_hi, x_ready, 1, 1, x_next)
            keep(0, 1)
            split_weight("cond")
            keep(0, 2)
            split_weight("gate")
            largest("attn")
            keep(0, 3)
            split_weight("value")
            split_weight("key")
            with pool.Fori(1, WINDOWS) as g:
                window(g)
            window(WINDOWS, gru=False)

        @block.vector
        def _(dve):
            def add_projection(dst, ps, w, name, proj, g, s, acc_sem, part, done):
                if s == 0:
                    dve.wait_ge(taken[name], halves(g, 1))
                dve.wait_ge(acc_sem, products(g, s))
                i = W16.index(w)
                dve.scalar_tensor_tensor(dst, ps[:, 1], unscale[:, i:i + 1], at_step(proj, s), ALU.mult, ALU.add)\
                    .then_inc(part, 1)
                dve.wait_ge(part, products(g, s))
                dve.scalar_tensor_tensor(dst, ps[:, 0], unscale[:, i:i + 1], dst, ALU.mult, ALU.add).then_inc(done, 1)

            def reset_pre(g, s):
                add_projection(rg, ps_r, "u_r", "rproj", rproj, g, s, r_acc, r_part, r_pre)

            def reset_mul(g, s):
                dve.wait_ge(r_sig, products(g, s))
                dve.tensor_tensor(rg, rg, state, ALU.mult).then_inc(rh_full, 1)

            def reset_split(g, s):
                n = products(g, s)
                dve.wait_ge(rh_full, n)
                dve.tensor_copy(rh_parts[:, 0], rg).then_inc(rh_hi, 1)
                dve.wait_ge(rh_hi, n)
                dve.tensor_tensor(rh_parts[:, 1], rg, rh_parts[:, 0], ALU.subtract).then_inc(rh_ready, 1)

            def reset(g, s):
                reset_pre(g, s)
                reset_mul(g, s)
                reset_split(g, s)

            def update(g, s):
                add_projection(zg, ps_z, "u_z", "zproj", zproj, g, s, z_acc, z_part, z_pre)

            def candidate_pre(g, s):
                add_projection(hc, ps_c, "u_h", "hproj", hproj, g, s, c_acc, c_part, c_pre)

            def blend(g, s):
                n = steps(g, s)
                dve.wait_ge(c_tanh, n)
                dve.tensor_tensor(hc, hc, zg, ALU.mult).then_inc(zc_done, 1)
                dve.wait_ge(zc_done, n)
                dve.wait_ge(kept_done, products(g, s))
                dve.scalar_tensor_tensor(state, hc, STATE_SCALE, kept, ALU.mult, ALU.add).then_inc(state_done, 1)
                split_state(s, n)

            def split_state(s, n):
                dve.wait_ge(state_done, n)
                dve.tensor_copy(hist[:, 0, :, s], state).then_inc(h_hi, 1)
                dve.wait_ge(h_hi, n)
                dve.tensor_tensor(hist[:, 1, :, s], state, hist[:, 0, :, s], ALU.subtract).then_inc(h_ready, 1)

            def new_state(g, s):
                candidate_pre(g, s)
                blend(g, s)

            def take_proj(name, g, h, dst, ps, v):
                dve.wait_ge(acc[name], halves(g, h))
                dve.tensor_tensor(by_time(half(dst, h)), by_time(ps[h]), over_time(half(cond_v[v], h)), ALU.add)\
                    .then_inc(taken[name], 1)

            def take_rproj(g, h):
                take_proj("rproj", g, h, rproj, ps_even, "c_r")

            def take_zproj(g, h):
                take_proj("zproj", g, h, zproj, ps_odd, "c_z")

            def take_hproj(g, h):
                take_proj("hproj", g, h, hproj, ps_odd, "c_h")

            def split_lo(dst, src, hi, done, q, h):
                dve.wait_ge(hi, halves(q, h))
                dve.tensor_tensor(half(dst[:, 1], h), half(src, h), half(dst[:, 0], h).bitcast(F32), ALU.subtract)\
                    .then_inc(done, 1)

            def style(q, h):
                dve.wait_ge(taken["attn"], halves(q, h))
                dve.wait_ge(res_in[h], 16 * (q + 1))
                dve.tensor_tensor(half(x2, h), half(x2, h), half(y_now, h), ALU.add).then_inc(x2_done, 1)
                dve.wait_ge(x2_done, halves(q, h))
                dve.tensor_tensor(by_time(half(y_now, h)), by_time(half(x2, h)), over_time(half(ys, h)), ALU.mult)\
                    .then_inc(xs_done, 1)

            def take_cond(q, h):
                dve.wait_ge(acc["cond"], halves(q, h))
                dve.tensor_tensor(by_time(half(y_now, h)), by_time(ps_even[h]), over_time(half(demod, h)), ALU.mult)\
                    .then_inc(taken["cond"], 1)

            def mix(q, h, mu, prev_tile, done):
                dve.wait_ge(taken["cond"], halves(q, h))
                for m in range(HALF * h, HALF * h + HALF):
                    dve.wait_ge(prev_tile, KT * q + m + 1)
                    d = dve.scalar_tensor_tensor(raw[:, m], y_now[:, m], vec[:, mu, m:m + 1], raw[:, m],
                                                 ALU.mult, ALU.add)
                d.then_inc(done, 1)

            def take_value(q, h):
                dve.wait_ge(acc["value"], halves(q, h))
                dve.wait_ge(taken["gate"], halves(q, h))
                dve.tensor_tensor(half(y_now, h), half(y_now, h), ps_odd[h][:, :, :], ALU.mult)\
                    .then_inc(taken["value"], 1)

            def residual(q, h):
                dve.wait_ge(taken["value"], halves(q, h))
                dve.tensor_tensor(half(x2, h), half(x2, h), half(y_now, h), ALU.add).then_inc(out_ready, 1)

            def demodulation():
                used_up(dve, "attn")
                dve.wait_ge(root_done, 1)
                dve.reciprocal(dinv, demod[:, :, :]).then_inc(demod_done, 1)
                dve.wait_ge(demod_done, 1)
                dve.tensor_tensor(dtmp, dinv, dinv, ALU.mult).then_inc(demod_done, 1)
                dve.wait_ge(demod_done, 2)
                dve.scalar_tensor_tensor(dtmp, ps_demod[:, :, :], EPS, dtmp, ALU.add, ALU.mult).then_inc(demod_done, 1)
                dve.wait_ge(demod_done, 3)
                dve.tensor_scalar(dtmp, dtmp, -0.5, 1.5, ALU.mult, ALU.add).then_inc(demod_done, 1)
                dve.wait_ge(demod_done, 4)
                dve.tensor_tensor(demod[:, :, :], dinv, dtmp, ALU.mult).then_inc(demod_done, 1)
                dve.wait_ge(demod_done, 5)

            def window(g, gru=True, proj=True, first=False):
                q = g - 1
                if gru:
                    reset(g, 0)
                    update(g, 0)
                if first:
                    demodulation()
                style(q, 0)
                if not gru:
                    split_lo(a_parts, y_now, xs_hi, xs_ready, q, 0)
                style(q, 1)
                if gru:
                    split_lo(a_parts, y_now, xs_hi, xs_ready, q, 0)
                split_lo(a_parts, y_now, xs_hi, xs_ready, q, 1)
                if gru:
                    take_hproj(g, 0)
                    take_hproj(g, 1)
                    new_state(g, 0)
                take_cond(q, 0)
                mix(q, 0, MU_K, prev_k_tile, mix_k)
                take_cond(q, 1)
                split_lo(b_parts, raw, xk_hi, xk_ready, q, 0)
                if gru:
                    reset_pre(g, 1)
                mix(q, 1, MU_K, prev_k_tile, mix_k)
                if gru:
                    reset_mul(g, 1)
                split_lo(b_parts, raw, xk_hi, xk_ready, q, 1)
                if gru:
                    reset_split(g, 1)
                mix(q, 0, MU_R, prev_r_tile, mix_r)
                if gru:
                    update(g, 1)
                split_lo(x_parts, raw, xr_hi, xr_ready, q, 0)
                if gru:
                    candidate_pre(g, 1)
                mix(q, 1, MU_R, prev_r_tile, mix_r)
                if gru:
                    blend(g, 1)
                if gru:
                    reset(g, 2)
                    update(g, 2)
                    new_state(g, 2)
                if proj:
                    split_lo(x_parts, raw, x_hi, x_ready, g + 1, 0)
                    split_lo(x_parts, raw, x_hi, x_ready, g + 1, 1)
                for h in range(2):
                    take_value(q, h)
                    if not gru:
                        residual(q, h)
                if gru:
                    reset(g, 3)
                    update(g, 3)
                if proj:
                    take_rproj(g + 1, 0)
                    take_rproj(g + 1, 1)
                if gru:
                    new_state(g, 3)
                if proj:
                    take_zproj(g + 1, 0)
                    take_zproj(g + 1, 1)

            def largest(name):
                i = W16.index(name)
                dve.tensor_reduce(wmax[:, i:i + 1], staged(dve, name).rearrange("p k m -> p (k m)"), AX_X, ALU.max,
                                  apply_absolute_value=True).then_inc(max_done, 1)

            def scale(name):
                i, n = W16.index(name), MAX_ORDER.index(name)
                dve.wait_ge(top_done, n + 1)
                dve.tensor_scalar(wtop[:, i:i + 1], wtop[:, i:i + 1], TINY, None, ALU.max).then_inc(pow_done, 1)
                dve.wait_ge(pow_done, 3 * n + 1)
                dve.tensor_scalar(wpow[:, i:i + 1].bitcast(U32), wtop[:, i:i + 1].bitcast(U32), EXPONENT, None,
                                  ALU.bitwise_and).then_inc(pow_done, 1)
                dve.wait_ge(pow_done, 3 * n + 2)
                dve.reciprocal(wrec[:, i:i + 1], wpow[:, i:i + 1]).then_inc(pow_done, 1)
                dve.wait_ge(pow_done, 3 * n + 3)
                dve.tensor_scalar(wscale[:, i:i + 1], wrec[:, i:i + 1], WEIGHT_TOP, None, ALU.mult).then_inc(scale_done, 1)
                dve.tensor_scalar(unscale[:, i:i + 1], wpow[:, i:i + 1], 1.0 / (WEIGHT_TOP * STATE_SCALE), None,
                                  ALU.mult).then_inc(scale_done, 1)

            def split_weight(name):
                w, w_split = staged(dve, name), wt[name]
                dve.wait_ge(w_hi, SPLIT_ORDER.index(name) + 1)
                if name in W16:
                    i = W16.index(name)
                    dve.wait_ge(scale_done, 2 * MAX_ORDER.index(name) + 2)
                    dve.scalar_tensor_tensor(w_split[:, 1].rearrange("p k m -> p (k m)"),
                                             w.rearrange("p k m -> p (k m)"), wscale[:, i:i + 1],
                                             w_split[:, 0].rearrange("p k m -> p (k m)"), ALU.mult, ALU.subtract)\
                        .then_inc(w_lo["dve"], 1)
                else:
                    dve.tensor_tensor(w_split[:, 1], w, w_split[:, 0].bitcast(F32), ALU.subtract).then_inc(w_lo["dve"], 1)

            dve.memset(zero[:, :], 0.0).then_inc(consts_done, 1)
            dve.memset(one[:, :], 1.0).then_inc(consts_done, 1)
            dve.memset(eps[:, :], EPS).then_inc(consts_done, 1)
            dve.wait_ge(small_in, 48)
            dve.tensor_scalar(rest[:, :, :], vec[:, :, :], -1.0, 1.0, ALU.mult, ALU.add).then_inc(consts_done, 1)
            dve.wait_ge(consts_done, 1)
            dve.tensor_tensor_scan(bias_sum, zero[0:1, :].broadcast_to([1, D]), bias_in, 0.0, ALU.add, ALU.add)\
                .then_inc(bias_done, 1)
            split_lo(x_parts, raw, x_hi, x_ready, 0, 0)
            split_lo(x_parts, raw, x_hi, x_ready, 0, 1)
            split_weight("w_z")
            dve.wait_ge(cgate_taken, WC.index("c_z") + 1)
            take_zproj(0, 0)
            take_zproj(0, 1)
            largest("u_r")
            scale("u_r")
            split_weight("u_r")
            largest("u_z")
            dve.wait_ge(cgate_taken, WC.index("c_h") + 1)
            take_hproj(0, 0)
            scale("u_z")
            take_hproj(0, 1)
            dve.tensor_scalar(ys[:, :, :], ys[:, :, :], YS_SCALE, None, ALU.mult).then_inc(ysq_done, 1)
            dve.wait_ge(ysq_done, 1)
            dve.tensor_tensor(ysq, ys[:, :, :], ys[:, :, :], ALU.mult).then_inc(ysq_done, 1)
            dve.wait_ge(z_sig, 1)
            dve.wait_ge(c_tanh, 1)
            dve.tensor_tensor(hc, hc, zg, ALU.mult).then_inc(zc_done, 1)
            dve.wait_ge(zc_done, 1)
            dve.tensor_scalar(state, hc, STATE_SCALE, None, ALU.mult).then_inc(state_done, 1)
            split_state(0, 1)
            largest("u_h")
            split_weight("u_z")
            scale("u_h")
            take_rproj(0, 0)
            take_rproj(0, 1)
            dve.wait_ge(taken["rproj"], halves(0, 1))
            reset(0, 1)
            split_weight("u_h")
            update(0, 1)
            w = staged(dve, "attn")
            for k in range(KT):
                dve.tensor_tensor_scan(w[:, k], zero[:, :].broadcast_to([P, D]), w[:, k], 0.0, ALU.add, ALU.add)\
                    .then_inc(scan_done, 1)
                if k == KT - 2:
                    new_state(0, 1)
            reset(0, 2)
            update(0, 2)
            new_state(0, 2)
            dve.wait_ge(scan_done, KT)
            largest("attn")
            reset(0, 3)
            update(0, 3)
            scale("attn")
            take_rproj(1, 0)
            take_rproj(1, 1)
            new_state(0, 3)
            split_weight("attn")
            take_zproj(1, 0)
            take_zproj(1, 1)
            dve.memset(yy[:, :, 0:B], 0.0).then_inc(cleared, 1)
            dve.wait_ge(cleared, 1)
            window(1, first=True)
            with dve.Fori(2, WINDOWS - 1) as g:
                window(g)
            window(WINDOWS - 1, proj=False)
            window(WINDOWS, gru=False, proj=False)


def kernel(**inputs):
    import concourse.bacc as bacc
    from concourse.bass_utils import run_bass_kernel_spmd as run

    f32 = {n: np.ascontiguousarray(a) for n, a in inputs.items()}

    def weight(name, turned=False):
        a = f32[name].T if turned else f32[name]
        return np.ascontiguousarray(a.reshape(KT, P, D).transpose(1, 0, 2))

    def columns(a):
        return a.reshape(KT, P, -1).transpose(1, 0, 2).reshape(P, -1)

    arrays = {
        "x": np.ascontiguousarray(f32["x"].reshape(B, WINDOWS, STEPS, KT, P).transpose(1, 4, 3, 2, 0).reshape(WINDOWS, P, KT, N)),
        "small": np.ascontiguousarray(np.concatenate(
            [columns(f32[n]) for n in ("L0_cond_b_r", "L0_cond_b_z", "L0_cond_b", "L0_ffn_mu_r", "L0_ffn_mu_k")]
            + [columns(f32["cond_1024"].T)], axis=1)),
        "bias_row": f32["L0_attn_bias"].reshape(1, D),
    }
    sources = {
        "c_r": ("L0_cond_C_r",), "c_z": ("L0_cond_C_z",), "c_h": ("L0_cond_C",),
        "u_r": ("L0_cond_U_r",), "u_z": ("L0_cond_U_z",), "u_h": ("L0_cond_U",),
        "w_r": ("L0_cond_W_r",), "w_z": ("L0_cond_W_z",), "w_h": ("L0_cond_W",),
        "cond": ("L0_cond2_weight",), "attn": ("L0_attn_W", True),
        "key": ("L0_ffn_W_k", True), "gate": ("L0_ffn_W_r", True), "value": ("L0_ffn_W_v", True),
    }
    for name, source in sources.items():
        arrays["raw_" + name] = weight(*source)

    nc = bacc.Bacc("TRN2", target_bir_lowering=False, num_devices=1)
    sources = {n: sources[n] for n in SLOT_OF if n in sources}
    dram = {n: nc.dram_tensor(n, a.shape, F32, kind="ExternalInput").ap() for n, a in arrays.items()}
    out = nc.dram_tensor("out", (WINDOWS, P, KT, N), F32, kind="ExternalOutput").ap()
    gru_ffn_kernel(nc, dram["x"], {n: dram["raw_" + n] for n in sources}, dram["small"], dram["bias_row"], out)
    r = run(nc, [arrays], core_ids=[0])
    y = np.asarray(r.results[0]["out"]).reshape(WINDOWS, P, KT, STEPS, B)
    return np.ascontiguousarray(y.transpose(4, 0, 3, 2, 1)).reshape(B, T, D)
```
